# Optimizing a Trainium2 kernel written in Bass

```python
import numpy as np
import jax
import jax.numpy as jnp

def _softmax(x, axis=-1):
    return jax.nn.softmax(x, axis=axis)

def _gelu(x):
    return jax.nn.gelu(x, approximate=True)

def _silu(x):
    return jax.nn.silu(x)

def _sigmoid(x):
    return jax.nn.sigmoid(x)

def _layernorm(x, axis=-1, eps=1e-05):
    m = jnp.mean(x, axis=axis, keepdims=True)
    v = jnp.var(x, axis=axis, keepdims=True)
    return (x - m) / jnp.sqrt(v + eps)

def _scatter_add(tgt, idx, src, axis=0):
    return tgt.at[idx].add(src)

def _segment_sum(src, seg, n):
    return jax.ops.segment_sum(src, seg, n)
kernel_name = 'mk_audio_tower_d1_tok_audfeat768_r4_4eade9'

def setup_inputs(seed: int=0):
    np.random.seed(seed)
    _w = jnp.asarray

    def _rec_inputs():
        import jax
        import jax.numpy as jnp
        _rk = jax.random.key(seed)
        x = -0.000183583 + 0.999963 * jax.random.normal(jax.random.fold_in(_rk, 1), (128, 125, 192), jnp.float32)
        return x
    x = _rec_inputs()

    def _L0_tok_setup():
        import jax, jax.numpy as jnp
        import numpy as np
        KEEP_RATIO = 0.7
        LN_EPS = 1e-05
        key = jax.random.key(seed)
        k1, k2 = jax.random.split(key)
        B, N, D = (16, 2048, 192)
        x = jax.random.normal(k1, (B, N, D), dtype=jnp.float32)
        gamma = jnp.ones((D,), dtype=jnp.float32)
        beta = jnp.zeros((D,), dtype=jnp.float32)
        w = jax.random.normal(k2, (D,), dtype=jnp.float32) * (1.0 / np.sqrt(D))
        b = jnp.zeros((1,), dtype=jnp.float32)
        return {'x': x, 'gamma': gamma, 'beta': beta, 'w': w, 'b': b}
    _L0_tok_all = _L0_tok_setup()
    _L0_tok_in = {k: v for k, v in _L0_tok_all.items() if k in ('gamma', 'beta', 'w', 'b')}
    del _L0_tok_all

    def _L0_attn_setup():
        import jax, jax.numpy as jnp
        import numpy as np
        HEADS = 12
        DIM_HEAD = 64
        SCALE = DIM_HEAD ** (-0.5)
        key = jax.random.key(seed)
        k1, k2, k3, k4 = jax.random.split(key, 4)
        dim, inner = (192, HEADS * DIM_HEAD)
        x = jax.random.normal(k1, (4, 512, dim), dtype=jnp.float32)
        w_qkv = jax.random.normal(k2, (dim, 3 * inner), dtype=jnp.float32) * dim ** (-0.5)
        w_out = jax.random.normal(k3, (inner, dim), dtype=jnp.float32) * inner ** (-0.5)
        b_out = jax.random.normal(k4, (dim,), dtype=jnp.float32) * 0.02
        return {'x': x, 'w_qkv': w_qkv, 'w_out': w_out, 'b_out': b_out}
    _L0_attn_all = _L0_attn_setup()
    _L0_attn_in = {k: v for k, v in _L0_attn_all.items() if k in ('w_qkv', 'w_out', 'b_out')}
    del _L0_attn_all

    def _L0_ffn_setup():
        import jax, jax.numpy as jnp
        import numpy as np
        B, S, H, I = (4, 512, 192, 384)
        E, K = (3, 2)
        INIT = 0.02

        def _expert(x, gw, uw, dw):
            return jax.nn.silu(x @ gw) * (x @ uw) @ dw
        key = jax.random.key(seed)
        ks = jax.random.split(key, 8)
        f32 = jnp.float32
        return {'x': jax.random.normal(ks[0], (B, S, H), f32), 'shared_gate': jax.random.normal(ks[1], (H, I), f32) * INIT, 'shared_up': jax.random.normal(ks[2], (H, I), f32) * INIT, 'shared_down': jax.random.normal(ks[3], (I, H), f32) * INIT, 'routed_gate': jax.random.normal(ks[4], (E, H, I), f32) * INIT, 'routed_up': jax.random.normal(ks[5], (E, H, I), f32) * INIT, 'routed_down': jax.random.normal(ks[6], (E, I, H), f32) * INIT, 'router_w': jax.random.normal(ks[7], (H, E), f32) * INIT, 'routing_bias': jnp.zeros((E,), f32)}
    _L0_ffn_all = _L0_ffn_setup()
    _L0_ffn_in = {k: v for k, v in _L0_ffn_all.items() if k in ('shared_gate', 'shared_up', 'shared_down', 'routed_gate', 'routed_up', 'routed_down', 'router_w', 'routing_bias')}
    del _L0_ffn_all
    return {'x': x, 'L0_tok_gamma': _L0_tok_in['gamma'], 'L0_tok_beta': _L0_tok_in['beta'], 'L0_tok_w': _L0_tok_in['w'], 'L0_tok_b': _L0_tok_in['b'], 'L0_attn_w_qkv': _L0_attn_in['w_qkv'], 'L0_attn_w_out': _L0_attn_in['w_out'], 'L0_attn_b_out': _L0_attn_in['b_out'], 'L0_ffn_shared_gate': _L0_ffn_in['shared_gate'], 'L0_ffn_shared_up': _L0_ffn_in['shared_up'], 'L0_ffn_shared_down': _L0_ffn_in['shared_down'], 'L0_ffn_routed_gate': _L0_ffn_in['routed_gate'], 'L0_ffn_routed_up': _L0_ffn_in['routed_up'], 'L0_ffn_routed_down': _L0_ffn_in['routed_down'], 'L0_ffn_router_w': _L0_ffn_in['router_w'], 'L0_ffn_routing_bias': _L0_ffn_in['routing_bias']}

def reference(x, L0_tok_gamma, L0_tok_beta, L0_tok_w, L0_tok_b, L0_attn_w_qkv, L0_attn_w_out, L0_attn_b_out, L0_ffn_shared_gate, L0_ffn_shared_up, L0_ffn_shared_down, L0_ffn_routed_gate, L0_ffn_routed_up, L0_ffn_routed_down, L0_ffn_router_w, L0_ffn_routing_bias):
    import jax
    import jax.numpy as jnp

    def _L0_tok_ref(x, gamma, beta, w, b):
        import jax, jax.numpy as jnp
        import numpy as np
        KEEP_RATIO = 0.7
        LN_EPS = 1e-05
        B, N, D = x.shape
        mu = jnp.mean(x, axis=-1, keepdims=True)
        var = jnp.mean(jnp.square(x - mu), axis=-1, keepdims=True)
        xn = (x - mu) * jax.lax.rsqrt(var + LN_EPS) * gamma + beta
        scores = jnp.einsum('bnd,d->bn', xn, w) + b[0]
        k = int(N * KEEP_RATIO)
        _, idx = jax.lax.top_k(scores, k)
        x_kept = jnp.take_along_axis(x, idx[..., None], axis=1)
        return x_kept

    def _L0_attn_ref(x, w_qkv, w_out, b_out):
        import jax, jax.numpy as jnp
        import numpy as np
        HEADS = 12
        DIM_HEAD = 64
        SCALE = DIM_HEAD ** (-0.5)
        B, N, _ = x.shape
        qkv = jnp.einsum('bnd,de->bne', x, w_qkv)
        q, k, v = jnp.split(qkv, 3, axis=-1)
        split_heads = lambda t: t.reshape(B, N, HEADS, DIM_HEAD).transpose(0, 2, 1, 3)
        q, k, v = (split_heads(q), split_heads(k), split_heads(v))
        dots = jnp.einsum('bhnd,bhmd->bhnm', q, k) * SCALE
        attn = jax.nn.softmax(dots, axis=-1)
        out = jnp.einsum('bhnm,bhmd->bhnd', attn, v)
        out = out.transpose(0, 2, 1, 3).reshape(B, N, HEADS * DIM_HEAD)
        return jnp.einsum('bne,ed->bnd', out, w_out) + b_out

    def _L0_ffn_ref(x, shared_gate, shared_up, shared_down, routed_gate, routed_up, routed_down, router_w, routing_bias):
        import jax, jax.numpy as jnp
        import numpy as np
        B, S, H, I = (4, 512, 192, 384)
        E, K = (3, 2)
        INIT = 0.02

        def _expert(x, gw, uw, dw):
            return jax.nn.silu(x @ gw) * (x @ uw) @ dw
        shared_out = _expert(x, shared_gate, shared_up, shared_down)
        routing_probs = jax.nn.sigmoid(x @ router_w + routing_bias)
        scores, indices = jax.lax.top_k(routing_probs, K)
        scores = scores / scores.sum(axis=-1, keepdims=True)
        combine_w = (jax.nn.one_hot(indices, E, dtype=x.dtype) * scores[..., None]).sum(axis=-2)
        g = jnp.einsum('bsh,ehi->ebsi', x, routed_gate)
        u = jnp.einsum('bsh,ehi->ebsi', x, routed_up)
        h = jax.nn.silu(g) * u
        out_e = jnp.einsum('ebsi,eih->ebsh', h, routed_down)
        combined = jnp.einsum('ebsh,bse->bsh', out_e, combine_w)
        return shared_out + combined
    h = _L0_tok_ref(x, L0_tok_gamma, L0_tok_beta, L0_tok_w, L0_tok_b)
    h = h + _L0_attn_ref(_layernorm(h, axis=-1), L0_attn_w_qkv, L0_attn_w_out, L0_attn_b_out)
    h = h + _L0_ffn_ref(_layernorm(h, axis=-1), L0_ffn_shared_gate, L0_ffn_shared_up, L0_ffn_shared_down, L0_ffn_routed_gate, L0_ffn_routed_up, L0_ffn_routed_down, L0_ffn_router_w, L0_ffn_routing_bias)
    return h

_drawn_inputs = setup_inputs


def setup_inputs(seed=0):
    import zlib

    import numpy as np

    out = dict(_drawn_inputs(seed))
    spreads = {'L0_tok_gamma': (1.0, 0.2), 'L0_tok_beta': (0.0, 0.1), 'L0_ffn_routing_bias': (0.0, 0.8)}
    factors = {'L0_attn_b_out': 3.045,
     'L0_ffn_shared_gate': 3.773,
     'L0_ffn_shared_up': 3.725,
     'L0_ffn_shared_down': 3.726,
     'L0_ffn_routed_gate': 5.333,
     'L0_ffn_routed_up': 5.284,
     'L0_ffn_routed_down': 5.302,
     'L0_ffn_router_w': 8.0}
    for name, (base, spread) in spreads.items():
        noise = np.random.default_rng([zlib.crc32(name.encode()), seed]).standard_normal(out[name].shape)
        drawn = base * np.exp(spread * noise) if base else spread * noise
        out[name] = jnp.asarray(drawn.astype(out[name].dtype))
    for name, factor in factors.items():
        out[name] = (out[name] * factor).astype(out[name].dtype)
    return out
```

```python
from contextlib import ExitStack

import concourse.bass as bass
from concourse import mybir

ALU = mybir.AluOpType
ACT = mybir.ActivationFunctionType
F32 = mybir.dt.float32
F32R = mybir.dt.float32r
I16 = mybir.dt.int16
AX_X = mybir.AxisListType.X

LN_EPS = 1e-5
HEADS = 12
DH = 64
TOPK = 2


class Group:

    def __init__(self, reg, off=0):
        self.reg, self.off = reg, off

    def __add__(self, n):
        return Group(self.reg, self.off + n)

    def count(self, per, k):
        fixed = self.off * per + k
        return fixed if self.reg is None else self.reg * per + fixed

    def index(self):
        return self.count(1, 0)


def wait(eng, sem, g, per, k):
    v = g.count(per, k)
    if not isinstance(v, int) or v > 0:
        eng.wait_ge(sem, v)


def wait_apart(eng, sem, g, per, k, passed):
    wait(eng, sem, g, per, k)
    eng.sem_inc(passed, 1)


def audio_tower_kernel(nc, x, gamma, beta, tok_w, tok_b, w_qkv, w_out, b_out, sh_gate, sh_up, sh_down,
                       rt_gate, rt_up, rt_down, router_w, routing_bias, out):
    B, N, D = x.shape
    KEEP = int(N * 0.7)
    GB = 4
    NG = B // GB
    TOK = GB * KEEP
    NT = 3
    TT = TOK // NT
    D1 = 128
    D2 = D - D1
    INNER = HEADS * DH
    E = rt_gate.shape[0]
    NE = E + 1
    I = sh_gate.shape[1]
    IC = I // 128
    HC = NE * IC
    QK = 2 * INNER // 128
    OC = INNER // 128
    HU = 4
    UNITS = GB * HEADS // HU
    PH = HEADS // 2
    VH = INNER // 2
    VW = DH + 1
    NPR = QK + 2 * GB
    WC = 3 * INNER + NE * 2 * I
    PIECE = 768
    NPQ = 3 * INNER // PIECE
    NPW = WC // PIECE
    SCALE = DH ** -0.5
    assert TOK % NT == 0 and TOK <= 512 and NE * IC == UNITS and 2 * I == PIECE and E == 3 and TOPK == 2

    PAIRS = [(b, t) for b in range(GB) for t in range(NT)
             if b * KEEP < (t + 1) * TT and (b + 1) * KEEP > t * TT]
    NP = len(PAIRS)

    with ExitStack() as ctx:
        def sb(name, shape, dt=F32):
            return ctx.enter_context(nc.sbuf_tensor(name, shape, dt))

        def sem(name):
            return ctx.enter_context(nc.semaphore(name))

        w_hi = sb("w_hi", [128, 2, WC], F32R)
        w_lo = sb("w_lo", [128, 2, WC], F32R)
        w_down = sb("w_down", [128, NE, IC, D])
        w_o = sb("w_o", [128, OC, D])
        w_router = sb("w_router", [128, 2, E])
        ident = sb("ident", [128, 128])
        earlier = sb("earlier", [N, N])
        place = sb("place", [N, NP, TT], I16)
        gw = sb("gw", [128, D])
        brow = sb("brow", [128, D])
        wrow = sb("wrow", [128, D])
        bias_o = sb("bias_o", [128, D])
        bias_r = sb("bias_r", [128, E])
        score0 = sb("score0", [128, 2])
        neg_half = sb("neg_half", [128, GB])
        xt = sb("xt", [N, GB, D])
        xc = sb("xc", [N, GB, D])
        bst = sb("bst", [N, GB, 6])
        mv = sb("mv", [N, GB, 2])
        rstd = sb("rstd", [N, GB])
        score = sb("score", [N, 2, GB])
        junk = sb("junk", [N, 2, N])
        rk = sb("rk", [N, 4, GB])
        mask = sb("mask", [N, NP, TT])
        h = sb("h", [TT, NT, D])
        hb = sb("hb", [TT, NT, D])
        h2 = sb("h2", [TT, NT, D])
        acc = sb("acc", [TT, NT, D])
        xn = sb("xn", [TT, NT, D])
        xs = sb("xs", [TT, NT, 3 * 128], F32R)
        lst = sb("lst", [TT, NT, 6])
        lmv = sb("lmv", [TT, NT, 2])
        lrs = sb("lrs", [TT, NT])
        xT = sb("xT", [128, 3, TOK], F32R)
        yT = sb("yT", [128, 3, TOK], F32R)
        qk = sb("qk", [128, QK, TOK])
        oT = qk[:, 0:OC, :]
        v1 = sb("v1", [KEEP, GB, HEADS, VW])
        def pairs_of(u):
            return [divmod(HU * (u // 2) + i, PH) for i in range(HU)]

        p = sb("p", [KEEP, 2, HU, KEEP])
        pT = sb("pT", [KEEP, 2, HU, KEEP])
        mx = sb("mx", [KEEP, 2, HU])
        rsum = sb("rsum", [KEEP, 2, HU])
        o = sb("o", [KEEP, GB * PH, 2 * DH])
        hT = sb("hT", [128, HC, TOK])
        th = sb("th", [128, 2, TOK])
        stage = hT[:, :, :].rearrange("p c n -> p (c n)")[:, 0:4 * PIECE].rearrange(
            "p (r a n) -> p r a n", r=2, a=2)
        z = sb("z", [TT, NT, E])
        ez = sb("ez", [TT, NT, E])
        pr = sb("pr", [TT, NT, E])
        cmp = sb("cmp", [TT, NT, 6])
        keep = sb("keep", [TT, NT, E])
        den = sb("den", [TT, NT, 2])
        rden = sb("rden", [TT, NT])
        cw = sb("cw", [TT, NT, E])

        ps = ctx.enter_context(nc.psum_tensor("ps", [128, 8, 512], F32))
        GU0 = 4

        names = """ld_const ld_bias ld_w0 ld_w1 ld_x st_out ld_small
            c_ident c_mask c_ones c_neg c_gw c_bw c_s0 w_his w_los_d w_los_p
            f_bn f_aggr f_eps f_rstd f_xc f_dot f_score f_bc f_rank f_rk f_mask
            sel hev hbs
            x_bn x_aggr x_eps x_rstd x_norm x_hi x_lo
            y_bn y_aggr y_eps y_rstd y_norm y_hi y_lo
            xt_pe xev_a xev_d prj prj_a prj_d
            s_pe smax ssub sexp t_pe pte pv_pe orec onm ot_pe oev_a oev_d wo_pe h2s
            yt_pe yev_a yev_d gate_pe up_pe tanhs silus hts dn_pe comb
            passed_d passed_p
            rt_pe rz rexp rone rprob rcmp rkeep rden_s cws""".split()
        S = {n: sem("s_" + n) for n in names}

        def bank(k, parts, cols):
            return ps[0:parts, k, 0:cols]

        TERMS = [("lo", 0, 0), ("hi", 0, 2), ("lo", 1, 1), ("hi", 1, 1), ("hi", 0, 0)]
        half = {"hi": w_hi, "lo": w_lo}
        CS = 4 * NT

        block = ctx.enter_context(nc.Block())

        @block.sync
        def _(sp):
            def bcast(dst, src, done):
                sp.dma_start(dst[:, :], src.partition_broadcast(128)).then_inc(S[done], 16)

            def load_x(g):
                v = g.index()
                src = x[v * GB:v * GB + GB] if isinstance(v, int) else x[bass.ds(v * GB, GB), :, :]
                sp.dma_start(xt[:, :, :], src.rearrange("b n d -> n b d")).then_inc(S["ld_x"], 16)

            def load_piece(k):
                if k >= 2:
                    if k - 2 < NPQ:
                        sp.wait_ge(S["w_los_d"], k - 1)
                    else:
                        sp.wait_ge(S["w_los_p"], k - 1 - NPQ)
                if k < NPQ:
                    parts = [(w_qkv[:, PIECE * k:PIECE * (k + 1)], 0, PIECE)]
                else:
                    e = k - NPQ
                    gt, up = (sh_gate, sh_up) if e == 0 else (rt_gate[e - 1], rt_up[e - 1])
                    parts = [(gt, 0, I), (up, I, 2 * I)]
                for w, a, b in parts:
                    sp.dma_start(stage[:, k % 2, 0, a:b], w[0:D1, :]).then_inc(S[f"ld_w{k % 2}"], 16)
                    sp.dma_start(stage[0:D2, k % 2, 1, a:b], w[D1:D, :]).then_inc(S[f"ld_w{k % 2}"], 16)
                    sp.dma_start(stage[D2:2 * D2, k % 2, 1, a:b], w[D1:D, :]).then_inc(S[f"ld_w{k % 2}"], 16)

            def store(g):
                sp.wait_ge(S["comb"], g.count(CS, CS))
                v = g.index()
                flat = out.rearrange("b k d -> (b k) d")
                dst = flat[v * TOK:(v + 1) * TOK] if isinstance(v, int) else flat[bass.ds(v * TOK, TOK), :]
                sp.dma_start(dst.rearrange("(t q) d -> q t d", t=NT), acc[:, :, :]).then_inc(S["st_out"], 16)

            load_x(Group(None))
            bcast(gw, gamma, "ld_const")
            bcast(wrow, tok_w, "ld_const")
            bcast(brow, beta, "ld_const")
            sp.dma_start(score0[:, 1:2], tok_b.partition_broadcast(128)).then_inc(S["ld_const"], 16)
            load_piece(0)
            load_piece(1)
            bcast(bias_o, b_out, "ld_bias")
            bcast(bias_r, routing_bias, "ld_bias")
            for k in range(2, NPQ):
                load_piece(k)
            sp.dma_start(w_o[:, :, :], w_out.rearrange("(c p) d -> p c d", p=128)).then_inc(S["ld_small"], 16)
            sp.dma_start(w_router[:, 0, :], router_w[0:D1, :]).then_inc(S["ld_small"], 16)
            sp.dma_start(w_router[0:D2, 1, :], router_w[D1:D, :]).then_inc(S["ld_small"], 16)
            sp.dma_start(w_router[D2:2 * D2, 1, :], router_w[D1:D, :]).then_inc(S["ld_small"], 16)
            sp.dma_start(w_down[:, 0, :, :], sh_down.rearrange("(c p) d -> p c d", p=128)).then_inc(S["ld_small"], 16)
            for e in range(E):
                sp.dma_start(w_down[:, e + 1, :, :],
                             rt_down[e].rearrange("(c p) d -> p c d", p=128)).then_inc(S["ld_small"], 16)
            sp.wait_ge(S["sel"], 2)
            load_x(Group(None, 1))
            for k in range(NPQ, NPW):
                load_piece(k)

            def step(g, ffn, nxt, nxt2):
                if nxt2:
                    wait(sp, S["sel"], g + 1, 2, 2)
                    load_x(g + 2)
                if ffn:
                    store(g + -1)

            step(Group(None), False, True, True)
            with sp.Fori(1, NG - 2) as i:
                step(Group(i), True, True, True)
            step(Group(None, NG - 2), True, True, False)
            step(Group(None, NG - 1), True, False, False)
            store(Group(None, NG - 1))
            sp.wait_ge(S["st_out"], 16 * NG)

        @block.tensor
        def _(pe):
            mm = nc.tensor.matmul

            def rank_rows(g):
                wait(pe, S["f_score"], g, 1, 1)
                wait(pe, S["xev_d"], g + -1, 1, 1)
                for b in range(GB):
                    last = mm(ps[0:N, 3, b * N:(b + 1) * N], score[:, 1, b:b + 1].to_broadcast([N, N]),
                              ident[0:N, 0:N], start=True, stop=True, is_transpose=True)
                last.then_inc(S["f_bc"], 1)

            def select(g):
                wait(pe, S["f_mask"], g, GB, GB)
                wait(pe, S["ld_x"], g, 16, 16)
                wait(pe, S["pte"], g, UNITS, 0)
                for t in range(NT):
                    if t == NT - 1:
                        wait(pe, S["onm"], g, UNITS, 0)
                    mine = [n for n, (b, u) in enumerate(PAIRS) if u == t]
                    dst = ps[0:TT, 2, t * D:(t + 1) * D] if t < NT - 1 else ps[0:TT, 3, 0:D]
                    for n in mine:
                        last = mm(dst, mask[:, n, :], xt[:, PAIRS[n][0], :], start=(n == mine[0]), stop=(n == mine[-1]))
                    if t >= NT - 2:
                        last.then_inc(S["sel"], 1)

            def to_features(banks, done):
                for k in range(3):
                    for t in range(NT):
                        last = mm(ps[:, banks[k], t * TT:(t + 1) * TT], xs[:, t, 128 * k:128 * (k + 1)].bitcast(F32),
                                  ident[0:TT, 0:TT], start=True, stop=True, is_transpose=True)
                    last.then_inc(done, 1)

            def tokens_to_features(g):
                wait(pe, S["x_hi"], g, 1, 1)
                wait(pe, S["x_lo"], g, 1, 1)
                wait(pe, S["oev_a"], g, OC // 2, 0)
                to_features((2, 3, 0), S["xt_pe"])

            def project(g, rows):
                wait(pe, S["xev_a"], g, 2, 2)
                wait(pe, S["xev_d"], g, 1, 1)
                for n in range(NPR):
                    bk = GU0 + n % 4
                    if n < 4:
                        wait(pe, S["comb"], g + -2, CS, CS)
                    else:
                        m = n - 4
                        wait(pe, S["prj_a" if m % 2 == 0 else "prj_d"], g, NPR // 2, m // 2 + 1)
                    if g.reg is None and g.off == 0:
                        k = min(n * 128 // PIECE, NPQ - 1)
                        if n in (0, PIECE // 128, QK):
                            pe.wait_ge(S["w_his"], k + 1)
                            pe.wait_ge(S["w_los_d"], k + 1)
                    if n < QK:
                        dst = bank(bk, 128, TOK)
                    else:
                        b, f = divmod(n - QK, 2)
                        dst = bank(bk, KEEP, VH)
                    for k, (hl, wc, xk) in enumerate(TERMS):
                        w = half[hl]
                        if n < QK:
                            last = mm(dst, w[:, wc, 128 * n:128 * (n + 1)], xT[:, xk, :], start=(k == 0), stop=(k == 4))
                        else:
                            c0 = 2 * INNER + VH * f
                            last = mm(dst, xT[:, xk, KEEP * b:KEEP * (b + 1)], w[:, wc, c0:c0 + VH],
                                      start=(k == 0), stop=(k == 4))
                    last.then_inc(S["prj"], 1)
                    if n == 5 and rows is not None:
                        rank_rows(rows)

            def scores(g, u):
                if u == 0:
                    wait(pe, S["prj_a"], g, NPR // 2, NPR // 2)
                    wait(pe, S["prj_d"], g, NPR // 2, NPR // 2)
                    wait(pe, S["yev_a"], g + -1, 2, 2)
                if u >= 2:
                    wait(pe, S["ssub"], g, UNITS, u - 1)
                r = DH * (u % 2)
                for i, (b, c) in enumerate(pairs_of(u)):
                    last = mm(ps[0:KEEP, u % 2, i * KEEP:(i + 1) * KEEP], qk[r:r + DH, c, KEEP * b:KEEP * (b + 1)],
                              qk[r:r + DH, QK // 2 + c, KEEP * b:KEEP * (b + 1)], start=True, stop=True)
                last.then_inc(S["s_pe"], 1)

            def transpose_p(g, u):
                wait(pe, S["sexp"], g, UNITS, u + 1)
                if u == 0:
                    wait(pe, S["rz"], g + -1, 1, 1)
                else:
                    wait(pe, S["pte"], g, UNITS, u)
                for k in range(HU):
                    last = mm(ps[0:KEEP, 2, k * KEEP:(k + 1) * KEEP], p[:, u % 2, k, :], ident[0:KEEP, 0:KEEP],
                              start=True, stop=True, is_transpose=True)
                last.then_inc(S["t_pe"], 1)

            def weigh_v(g, u, ranked=False):
                wait(pe, S["pte"], g, UNITS, u + 1)
                if u == 0 and ranked:
                    wait(pe, S["f_rank"], g + 1, 2 * GB, 2 * GB)
                if u > 0:
                    wait(pe, S["onm"], g, UNITS, u)
                for i, (b, c) in enumerate(pairs_of(u)):
                    last = mm(ps[0:KEEP, 3, i * VW:(i + 1) * VW], pT[:, u % 2, i, :], v1[:, b, 2 * c + u % 2, :],
                              start=True, stop=True)
                last.then_inc(S["pv_pe"], 1)

            def gate_up(g, c, projected):
                if c == 0:
                    wait(pe, S["yev_a"], g, 2, 2)
                    wait(pe, S["yev_d"], g, 1, 1)
                    if g.reg is None and g.off == 0:
                        pe.wait_ge(S["w_his"], NPW)
                        pe.wait_ge(S["w_los_p"], NPW - NPQ)
                if c == 0 and projected:
                    wait(pe, S["prj_a"], g + 1, NPR // 2, NPR // 2)
                    wait(pe, S["prj_d"], g + 1, NPR // 2, NPR // 2)
                if c == 0 and not projected:
                    wait(pe, S["comb"], g, CS, 0)
                if c >= 2:
                    wait(pe, S["hts"], g, HC, c - 1)
                e, ic = divmod(c, IC)
                for up in range(2):
                    dst = bank(GU0 + 2 * (c % 2) + up, 128, TOK)
                    c0 = 3 * INNER + e * 2 * I + up * I + 128 * ic
                    for k, (hl, wc, xk) in enumerate(TERMS):
                        last = mm(dst, half[hl][:, wc, c0:c0 + 128], yT[:, xk, :], start=(k == 0), stop=(k == 4))
                    last.then_inc(S["up_pe" if up else "gate_pe"], 1)

            def down(g, n):
                t, pair = divmod(n, 2)
                if n == 0:
                    wait(pe, S["hts"], g, HC, HC)
                    if g.reg is None and g.off == 0:
                        pe.wait_ge(S["ld_small"], 16 * (4 + NE))
                if n >= 4:
                    wait(pe, S["comb"], g, CS, 2 * (n - 3))
                for e in range(2):
                    for c in range(IC):
                        ex = 2 * pair + e
                        last = mm(ps[0:TT, GU0 + n % 4, D * e:D * (e + 1)], hT[:, ex * IC + c, TT * t:TT * (t + 1)],
                                  w_down[:, ex, c, :], start=(c == 0), stop=(c == IC - 1))
                last.then_inc(S["dn_pe"], 1)

            def out_to_features(g, c):
                if c == 0:
                    wait(pe, S["onm"], g, UNITS, UNITS)
                    wait(pe, S["ssub"], g, UNITS, UNITS)
                if c >= 2:
                    wait(pe, S["oev_a" if c % 2 == 0 else "oev_d"], g, OC // 2, c // 2)
                for b in range(GB):
                    last = mm(ps[:, c % 2, KEEP * b:KEEP * (b + 1)], o[:, b * PH + c, :],
                              ident[0:KEEP, 0:KEEP], start=True, stop=True, is_transpose=True)
                last.then_inc(S["ot_pe"], 1)

            def project_out(g, nxt):
                wait(pe, S["oev_a"], g, OC // 2, OC // 2)
                wait(pe, S["oev_d"], g, OC // 2, OC // 2)
                if nxt:
                    wait(pe, S["xev_a"], g + 1, 2, 1)
                if g.reg is None and g.off == 0:
                    pe.wait_ge(S["ld_small"], 16 * (4 + NE))
                for t in range(NT):
                    dst = ps[0:TT, 1, t * D:(t + 1) * D] if t < NT - 1 else ps[0:TT, 2, 0:D]
                    for c in range(OC):
                        last = mm(dst, oT[:, c, TT * t:TT * (t + 1)], w_o[:, c, :], start=(c == 0), stop=(c == OC - 1))
                    if t >= NT - 2:
                        last.then_inc(S["wo_pe"], 1)

            def experts_to_features(g):
                wait(pe, S["y_hi"], g, 1, 1)
                wait(pe, S["y_lo"], g, 1, 1)
                to_features((0, 2, 1), S["yt_pe"])

            def router(g):
                wait(pe, S["yev_a"], g, 2, 2)
                wait(pe, S["yev_d"], g, 1, 1)
                for t in range(NT):
                    for k, (yk, wk) in enumerate(((2, 0), (1, 1), (0, 0))):
                        last = mm(ps[0:TT, 2, 4 * t:4 * t + E],
                                  yT[:, yk, TT * t:TT * (t + 1)].bitcast(F32),
                                  w_router[:, wk, :], start=(k == 0), stop=(k == 2))
                last.then_inc(S["rt_pe"], 1)

            def step(g, ffn, nxt, nxt2, attn=True):
                for s in range(UNITS + 1):
                    if attn and s < UNITS:
                        scores(g, s)
                    if ffn and s < UNITS:
                        gate_up(g + -1, s, attn)
                    if attn and s >= 1:
                        transpose_p(g, s - 1)
                    if attn and s >= 2:
                        weigh_v(g, s - 2, nxt)
                if ffn:
                    down(g + -1, 0)
                if attn:
                    weigh_v(g, UNITS - 1)
                if nxt:
                    select(g + 1)
                for c in range(OC):
                    if attn:
                        out_to_features(g, c)
                    if ffn and c + 1 < 2 * NT:
                        down(g + -1, c + 1)
                if nxt:
                    tokens_to_features(g + 1)
                if attn:
                    project_out(g, nxt)
                if nxt:
                    project(g + 1, g + 2 if nxt2 else None)
                if attn:
                    experts_to_features(g)
                    router(g)

            pe.wait_ge(S["c_ident"], 2)
            first = Group(None)
            rank_rows(first)
            select(first)
            tokens_to_features(first)
            project(first, first + 1)
            step(first, False, True, True)
            with pe.Fori(1, NG - 2) as i:
                step(Group(i), True, True, True)
            step(Group(None, NG - 2), True, True, False)
            step(Group(None, NG - 1), True, False, False)
            step(Group(None, NG), True, False, False, attn=False)

        @block.scalar
        def _(act):
            af = nc.scalar.activation

            def split_weights(k):
                loads = sum(3 if m < NPQ else 6 for m in range(k % 2, k + 1, 2))
                act.wait_ge(S[f"ld_w{k % 2}"], 16 * loads)
                af(w_hi[:, :, PIECE * k:PIECE * (k + 1)], stage[:, k % 2, :, :], ACT.Copy).then_inc(S["w_his"], 1)

            def copy_selected(g):
                wait(act, S["sel"], g, 2, 1)
                wait(act, S["hbs"], g, 1, 0)
                af(h[:, 0:2, :], ps[0:TT, 2, 0:2 * D].rearrange("q (t d) -> q t d", t=2), ACT.Copy).then_inc(S["hev"], 1)
                wait(act, S["sel"], g, 2, 2)
                af(h[:, 2, :], ps[0:TT, 3, 0:D], ACT.Copy).then_inc(S["hev"], 1)

            def high_part_tokens(g):
                wait(act, S["x_norm"], g, 1, 1)
                wait(act, S["yt_pe"], g + -1, 3, 0)
                af(xs[:, :, 0:D], xn[:, :, :], ACT.Copy).then_inc(S["x_hi"], 1)

            def high_part_experts(g, nxt):
                wait(act, S["y_norm"], g, 1, 1)
                if nxt:
                    wait(act, S["xt_pe"], g + 1, 3, 3)
                af(xs[:, :, 0:D], xn[:, :, :], ACT.Copy).then_inc(S["y_hi"], 1)

            def features(dst, k, bk, src, g, done):
                wait(act, src, g, 3, k + 1)
                af(dst[:, k, :], bank(bk, 128, TOK), ACT.Copy).then_inc(done, 1)

            def projected(g, n):
                wait(act, S["prj"], g, NPR, n + 1)
                if n < QK:
                    af(qk[:, n, :], bank(GU0 + n % 4, 128, TOK), ACT.Copy).then_inc(S["prj_a"], 1)
                else:
                    b, f = divmod(n - QK, 2)
                    af(v1[:, b, f * 6:f * 6 + 6, 0:DH],
                       bank(GU0 + n % 4, KEEP, VH).rearrange("q (a d) -> q a d", d=DH), ACT.Copy).then_inc(S["prj_a"], 1)

            def exponentials(g, u):
                wait(act, S["ssub"], g, UNITS, u + 1)
                v = p[:, u % 2, :, :]
                af(v, v, ACT.Exp, scale=SCALE).then_inc(S["sexp"], 1)

            def copy_pT(g, u):
                wait(act, S["t_pe"], g, UNITS, u + 1)
                if u >= 2:
                    wait(act, S["pv_pe"], g, UNITS, u - 1)
                af(pT[:, u % 2, :, :], bank(2, KEEP, HU * KEEP).rearrange("q (a n) -> q a n", a=HU),
                   ACT.Copy).then_inc(S["pte"], 1)

            def tanh_gate(g, c):
                wait(act, S["gate_pe"], g, HC, c + 1)
                if c >= 2:
                    wait(act, S["hts"], g, HC, c - 1)
                af(th[:, c % 2, :], bank(GU0 + 2 * (c % 2), 128, TOK), ACT.Tanh, scale=0.5).then_inc(S["tanhs"], 1)

            def out_features(g, c):
                wait(act, S["ot_pe"], g, OC, c + 1)
                af(oT[:, c, :], bank(c % 2, 128, TOK), ACT.Copy).then_inc(S["oev_a"], 1)

            def router_exp(g):
                wait(act, S["rz"], g, 1, 1)
                af(ez[:, :, :], z[:, :, :], ACT.Exp, scale=-1.0).then_inc(S["rexp"], 1)

            def step(g, ffn, nxt, nxt2, attn=True):
                for s in range(UNITS + 1):
                    if attn and s < UNITS:
                        exponentials(g, s)
                    if ffn and s < UNITS:
                        tanh_gate(g + -1, s)
                    if attn and s >= 1:
                        copy_pT(g, s - 1)
                if nxt:
                    copy_selected(g + 1)
                if attn:
                    out_features(g, 0)
                    out_features(g, 2)
                if nxt:
                    high_part_tokens(g + 1)
                if attn:
                    out_features(g, 4)
                if nxt:
                    features(xT, 0, 2, S["xt_pe"], g + 1, S["xev_a"])
                    features(xT, 2, 0, S["xt_pe"], g + 1, S["xev_a"])
                    for n in range(0, 6, 2):
                        projected(g + 1, n)
                if attn:
                    high_part_experts(g, nxt)
                if nxt:
                    for n in range(6, NPR, 2):
                        projected(g + 1, n)
                if attn:
                    features(yT, 0, 0, S["yt_pe"], g, S["yev_a"])
                    features(yT, 2, 1, S["yt_pe"], g, S["yev_a"])
                    router_exp(g)

            first = Group(None)
            for k in range(NPQ):
                split_weights(k)
            copy_selected(first)
            high_part_tokens(first)
            features(xT, 0, 2, S["xt_pe"], first, S["xev_a"])
            features(xT, 2, 0, S["xt_pe"], first, S["xev_a"])
            for n in range(0, NPR, 2):
                projected(first, n)
            for k in range(NPQ, NPW):
                split_weights(k)
            step(first, False, True, True)
            with act.Fori(1, NG - 2) as i:
                step(Group(i), True, True, True)
            step(Group(None, NG - 2), True, True, False)
            step(Group(None, NG - 1), True, False, False)
            step(Group(None, NG), True, False, False, attn=False)

        @block.vector
        def _(dve):
            v = nc.vector

            def split_low(k):
                dve.wait_ge(S["w_his"], k + 1)
                v.tensor_tensor(w_lo[:, :, PIECE * k:PIECE * (k + 1)], stage[:, k % 2, :, :],
                                w_hi[:, :, PIECE * k:PIECE * (k + 1)].bitcast(F32), ALU.subtract).then_inc(S["w_los_d"], 1)

            def score_stats(g):
                wait(dve, S["ld_x"], g, 16, 16)
                for b in range(GB):
                    v.bn_stats(bst[:, b, :], xt[:, b, :]).then_inc(S["f_bn"], 1)
                wait(dve, S["f_bn"], g, GB, GB)
                wait_apart(dve, S["f_xc"], g, GB, 0, S["passed_d"])
                for b in range(GB):
                    v.bn_aggr(mv[:, b, :], bst[:, b, :]).then_inc(S["f_aggr"], 1)

            def score_dots(g):
                for b in range(GB):
                    wait(dve, S["f_xc"], g, GB, b + 1)
                    v.tensor_tensor_reduce(out=xc[:, b, :], in0=xc[:, b, :], in1=gw[0:N, :], scale=1.0, scalar=0.0,
                                           op0=ALU.mult, op1=ALU.add, accum_out=score[:, 0, b:b + 1]).then_inc(S["f_dot"], 1)
                wait(dve, S["f_dot"], g, GB, GB)
                v.tensor_scalar(score[:, 1, :], score[:, 0, :], score0[0:N, 0:1], None, ALU.add).then_inc(S["f_score"], 1)

            def rank(g, b):
                wait(dve, S["f_bc"], g, 1, 1)
                row = ps[0:N, 3, b * N:(b + 1) * N]
                s = score[:, 1, b:b + 1]
                wait(dve, S["f_rank"], g, 2 * GB, 2 * b - 1)
                v.tensor_scalar(junk[:, 0, :], row, s, None, ALU.is_gt, ALU.add,
                                accum_out=rk[:, 0, b:b + 1]).then_inc(S["f_rank"], 1)
                wait(dve, S["f_rank"], g, 2 * GB, 2 * b)
                v.scalar_tensor_tensor(out=junk[:, 1, :], in0=row, scalar=s, in1=earlier[:, :], op0=ALU.is_equal,
                                       op1=ALU.mult, accum_out=rk[:, 1, b:b + 1]).then_inc(S["f_rank"], 1)

            def masks(g):
                wait(dve, S["f_rank"], g, 2 * GB, 2 * GB)
                v.tensor_tensor(rk[:, 2, :], rk[:, 0, :], rk[:, 1, :], ALU.add).then_inc(S["f_rk"], 1)
                wait(dve, S["f_rk"], g, 3, 1)
                v.tensor_scalar(rk[:, 3, :], rk[:, 2, :], float(KEEP), 4096.0, ALU.is_ge, ALU.mult).then_inc(S["f_rk"], 1)
                wait(dve, S["f_rk"], g, 3, 2)
                v.tensor_tensor(rk[:, 3, :], rk[:, 3, :], rk[:, 2, :], ALU.add).then_inc(S["f_rk"], 1)
                wait(dve, S["f_rk"], g, 3, 3)
                wait(dve, S["sel"], g, 2, 0)
                for b in range(GB):
                    mine = [n for n, (c, t) in enumerate(PAIRS) if c == b]
                    a, z_ = mine[0], mine[-1] + 1
                    v.tensor_scalar(mask[:, a:z_, :], place[:, a:z_, :], rk[:, 3, b:b + 1], None,
                                    ALU.is_equal).then_inc(S["f_mask"], 1)

            def ln_stats(src, g, k):
                for t in range(NT):
                    v.bn_stats(lst[:, t, :], src[:, t, :]).then_inc(S[k + "_bn"], 1)
                wait_apart(dve, S[k + "_bn"], g, NT, NT, S["passed_d"])
                for t in range(NT):
                    v.bn_aggr(lmv[:, t, :], lst[:, t, :]).then_inc(S[k + "_aggr"], 1)

            def normalise(src, g, k, other, split):
                wait(dve, S[k + "_rstd"], g, 1, 1)
                wait(dve, S[other + "_hi"], split, 1, 1)
                wait(dve, S[other + "_lo"], split, 1, 1)
                for t in range(NT):
                    last = v.tensor_scalar(xn[:, t, :], src[:, t, :], lmv[:, t, 0:1], lrs[:, t:t + 1],
                                           ALU.subtract, ALU.mult)
                last.then_inc(S[k + "_norm"], 1)

            def features(dst, bk, src, g, done):
                wait(dve, src, g, 3, 2)
                v.tensor_copy(dst[:, 1, :], bank(bk, 128, TOK)).then_inc(done, 1)

            def projected(g, n):
                wait(dve, S["prj"], g, NPR, n + 1)
                if n < QK:
                    v.tensor_copy(qk[:, n, :], bank(GU0 + n % 4, 128, TOK)).then_inc(S["prj_d"], 1)
                else:
                    b, f = divmod(n - QK, 2)
                    v.tensor_copy(v1[:, b, f * 6:f * 6 + 6, 0:DH],
                                  bank(GU0 + n % 4, KEEP, VH).rearrange("q (a d) -> q a d", d=DH)).then_inc(S["prj_d"], 1)

            def shift_scores(g, u):
                s = bank(u % 2, KEEP, HU * KEEP).rearrange("q (a m) -> q a m", a=HU)
                m = mx[:, u % 2, :]
                wait(dve, S["s_pe"], g, UNITS, u + 1)
                v.tensor_reduce(m, s, AX_X, ALU.max).then_inc(S["smax"], 1)
                wait(dve, S["smax"], g, UNITS, u + 1)
                if u >= 2:
                    wait(dve, S["t_pe"], g, UNITS, u - 1)
                v.tensor_tensor(p[:, u % 2, :, :], s, m.unsqueeze(2).to_broadcast([KEEP, HU, KEEP]),
                                ALU.subtract).then_inc(S["ssub"], 1)

            def normalise_out(g, u):
                wait(dve, S["pv_pe"], g, UNITS, u + 1)
                s = bank(3, KEEP, HU * VW).rearrange("q (a d) -> q a d", a=HU)
                r = rsum[:, u % 2, :]
                v.reciprocal(r, s[:, :, DH]).then_inc(S["orec"], 1)
                wait(dve, S["orec"], g, UNITS, u + 1)
                if u == 0:
                    wait(dve, S["ot_pe"], g, OC, 0)
                k = HU * (u // 2)
                v.tensor_tensor(o[:, k:k + HU, DH * (u % 2):DH * (u % 2 + 1)], s[:, :, 0:DH], r.unsqueeze(2).to_broadcast([KEEP, HU, DH]),
                                ALU.mult).then_inc(S["onm"], 1)

            def hidden(g, c):
                wait(dve, S["tanhs"], g, HC, c + 1)
                t = th[:, c % 2, :]
                v.scalar_tensor_tensor(out=t, in0=t, scalar=1.0, in1=bank(GU0 + 2 * (c % 2), 128, TOK), op0=ALU.add,
                                       op1=ALU.mult).then_inc(S["silus"], 1)
                wait(dve, S["silus"], g, HC, c + 1)
                wait(dve, S["up_pe"], g, HC, c + 1)
                v.scalar_tensor_tensor(out=hT[:, c, :], in0=t, scalar=0.5, in1=bank(GU0 + 2 * (c % 2) + 1, 128, TOK),
                                       op0=ALU.mult, op1=ALU.mult).then_inc(S["hts"], 1)

            def out_features(g, c):
                wait(dve, S["ot_pe"], g, OC, c + 1)
                v.tensor_copy(oT[:, c, :], bank(c % 2, 128, TOK)).then_inc(S["oev_d"], 1)

            def combine(g, n):
                t, pair = divmod(n, 2)
                if n == 0:
                    wait(dve, S["cws"], g, 1, 1)
                    wait(dve, S["st_out"], g, 16, 0)
                wait(dve, S["dn_pe"], g, 2 * NT, n + 1)
                bk = ps[0:TT, GU0 + n % 4, :]
                a = acc[:, t, :]

                def mine(k):
                    wait(dve, S["comb"], g, CS, 4 * t + k)
                if pair == 0:
                    v.tensor_tensor(a, bk[:, 0:D], h2[:, t, :], ALU.add).then_inc(S["comb"], 1)
                    mine(1)
                    v.scalar_tensor_tensor(out=a, in0=bk[:, D:2 * D], scalar=cw[:, t, 0:1], in1=a, op0=ALU.mult,
                                           op1=ALU.add).then_inc(S["comb"], 1)
                else:
                    mine(2)
                    v.scalar_tensor_tensor(out=a, in0=bk[:, 0:D], scalar=cw[:, t, 1:2], in1=a, op0=ALU.mult,
                                           op1=ALU.add).then_inc(S["comb"], 1)
                    mine(3)
                    v.scalar_tensor_tensor(out=a, in0=bk[:, D:2 * D], scalar=cw[:, t, 2:3], in1=a, op0=ALU.mult,
                                           op1=ALU.add).then_inc(S["comb"], 1)

            def residual(g):
                wait(dve, S["hbs"], g, 1, 1)
                wait(dve, S["wo_pe"], g, 2, 1)
                v.tensor_tensor(h2[:, 0:2, :], ps[0:TT, 1, 0:2 * D].rearrange("q (t d) -> q t d", t=2), hb[:, 0:2, :],
                                ALU.add).then_inc(S["h2s"], 1)
                wait(dve, S["wo_pe"], g, 2, 2)
                v.tensor_tensor(h2[:, 2, :], ps[0:TT, 2, 0:D], hb[:, 2, :], ALU.add).then_inc(S["h2s"], 1)
                wait(dve, S["h2s"], g, 2, 2)

            def router_logits(g):
                wait(dve, S["rt_pe"], g, 1, 1)
                v.tensor_tensor(z[:, :, :], ps[0:TT, 2, 0:4 * NT].rearrange("q (t e) -> q t e", e=4)[:, :, 0:E],
                                bias_r[0:TT, :].unsqueeze(1).to_broadcast([TT, NT, E]), ALU.add).then_inc(S["rz"], 1)

            def router_probs(g):
                wait(dve, S["rexp"], g, 1, 1)
                v.tensor_scalar(ez[:, :, :], ez[:, :, :], 1.0, None, ALU.add).then_inc(S["rone"], 1)
                wait(dve, S["rone"], g, 1, 1)
                v.reciprocal(pr[:, :, :], ez[:, :, :]).then_inc(S["rprob"], 1)

            def router_share(g):
                wait(dve, S["rkeep"], g, 4, 4)
                v.reciprocal(rden[:, :], den[:, :, 1]).then_inc(S["rden_s"], 1)

            def step(g, ffn, nxt, nxt2, attn=True):
                for s in range(UNITS + 1):
                    if attn and s < UNITS:
                        shift_scores(g, s)
                    if attn and s == 1 and (g.reg is not None or g.off > 0):
                        router_probs(g + -1)
                    if attn and s == 4 and (g.reg is not None or g.off > 0):
                        router_share(g + -1)
                    if not attn and s == 0:
                        router_probs(g + -1)
                        router_share(g + -1)
                    if attn and s >= 3:
                        normalise_out(g, s - 3)
                    if ffn and s < UNITS:
                        hidden(g + -1, s)
                if attn:
                    normalise_out(g, UNITS - 2)
                    normalise_out(g, UNITS - 1)
                if ffn:
                    combine(g + -1, 0)
                if nxt:
                    wait(dve, S["hev"], g + 1, 2, 2)
                    ln_stats(h, g + 1, "x")
                if attn:
                    out_features(g, 1)
                if ffn:
                    combine(g + -1, 1)
                if nxt:
                    normalise(h, g + 1, "x", "y", g + -1)
                if ffn:
                    combine(g + -1, 2)
                if attn:
                    out_features(g, 3)
                if ffn:
                    combine(g + -1, 3)
                if nxt2:
                    score_stats(g + 2)
                if ffn:
                    combine(g + -1, 4)
                if attn:
                    out_features(g, 5)
                if ffn:
                    combine(g + -1, 5)
                if nxt:
                    features(xT, 3, S["xt_pe"], g + 1, S["xev_d"])
                if nxt2:
                    score_dots(g + 2)
                if attn:
                    residual(g)
                    ln_stats(h2, g, "y")
                if nxt:
                    projected(g + 1, 1)
                    projected(g + 1, 3)
                if attn:
                    normalise(h2, g, "y", "x", g + 1 if nxt else g)
                if nxt:
                    for n in range(5, NPR, 2):
                        projected(g + 1, n)
                        if nxt2 and n in (7, 9, 11, 13):
                            rank(g + 2, (n - 7) // 2)
                        if nxt2 and n == 15:
                            masks(g + 2)
                if attn:
                    features(yT, 2, S["yt_pe"], g, S["yev_d"])
                    router_logits(g)

            dve.wait_ge(S["ld_const"], 16 * 4)
            v.tensor_tensor(gw[:, :], gw[:, :], wrow[:, :], ALU.mult).then_inc(S["c_gw"], 1)
            v.tensor_tensor_reduce(out=brow[:, :], in0=brow[:, :], in1=wrow[:, :], scale=1.0, scalar=0.0, op0=ALU.mult,
                                   op1=ALU.add, accum_out=score0[:, 0:1]).then_inc(S["c_bw"], 1)
            dve.wait_ge(S["c_bw"], 1)
            v.tensor_tensor(score0[:, 0:1], score0[:, 0:1], score0[:, 1:2], ALU.add).then_inc(S["c_s0"], 1)
            first = Group(None)
            dve.wait_ge(S["ld_bias"], 32)
            dve.wait_ge(S["c_gw"], 1)
            dve.wait_ge(S["c_s0"], 1)
            score_stats(first)
            split_low(0)
            score_dots(first)
            split_low(1)
            dve.wait_ge(S["c_mask"], 2 + NP)
            for b in range(GB):
                rank(first, b)
            masks(first)
            for k in range(2, NPQ):
                split_low(k)
            dve.wait_ge(S["hev"], 2)
            ln_stats(h, first, "x")
            normalise(h, first, "x", "y", first + -1)
            score_stats(first + 1)
            features(xT, 3, S["xt_pe"], first, S["xev_d"])
            score_dots(first + 1)
            for n in range(1, NPR, 2):
                projected(first, n)
                if n in (7, 9, 11, 13):
                    rank(first + 1, (n - 7) // 2)
                if n == 15:
                    masks(first + 1)
            step(first, False, True, True)
            with dve.Fori(1, NG - 2) as i:
                step(Group(i), True, True, True)
            step(Group(None, NG - 2), True, True, False)
            step(Group(None, NG - 1), True, False, False)
            step(Group(None, NG), True, False, False, attn=False)

        @block.gpsimd
        def _(pool):
            q = nc.gpsimd

            q.memset(ident[:, :], 0.0).then_inc(S["c_ident"], 1)
            q.memset(earlier[:, :], 1.0).then_inc(S["c_mask"], 1)
            q.memset(neg_half[:, :], -0.5).then_inc(S["c_neg"], 1)
            pool.wait_ge(S["c_ident"], 1)
            q.affine_select(out=ident[:, :], in_=ident[:, :], compare_op=ALU.not_equal, fill=1.0, base=0,
                            pattern=[[-1, 128]], channel_multiplier=1).then_inc(S["c_ident"], 1)
            pool.wait_ge(S["c_mask"], 1)
            q.affine_select(out=earlier[:, :], in_=earlier[:, :], compare_op=ALU.is_gt, fill=0.0, base=0,
                            pattern=[[-1, N]], channel_multiplier=1).then_inc(S["c_mask"], 1)
            for n, (b, t) in enumerate(PAIRS):
                q.iota(place[:, n, :], pattern=[[1, TT]], base=TT * t - KEEP * b,
                       channel_multiplier=0).then_inc(S["c_mask"], 1)
            for b in range(GB):
                q.memset(v1[:, b, :, DH], 1.0).then_inc(S["c_ones"], 1)
            pool.wait_ge(S["c_neg"], 1)

            def score_norm(g):
                wait_apart(pool, S["f_aggr"], g, GB, GB, S["passed_p"])
                q.tensor_scalar(rstd[:, :], mv[:, :, 1], LN_EPS, None, ALU.add).then_inc(S["f_eps"], 1)
                wait(pool, S["f_eps"], g, 1, 1)
                q.tensor_tensor(rstd[:, :], rstd[:, :], neg_half[0:N, 0:GB], ALU.pow).then_inc(S["f_rstd"], 1)
                wait(pool, S["f_rstd"], g, 1, 1)
                wait_apart(pool, S["f_dot"], g, GB, 0, S["passed_p"])
                for b in range(GB):
                    q.tensor_scalar(xc[:, b, :], xt[:, b, :], mv[:, b, 0:1], rstd[:, b:b + 1], ALU.subtract,
                                    ALU.mult).then_inc(S["f_xc"], 1)

            def ln_rstd(g, k):
                wait_apart(pool, S[k + "_aggr"], g, NT, NT, S["passed_p"])
                q.tensor_scalar(lrs[:, :], lmv[:, :, 1], LN_EPS, None, ALU.add).then_inc(S[k + "_eps"], 1)
                wait(pool, S[k + "_eps"], g, 1, 1)
                q.tensor_tensor(lrs[:, :], lrs[:, :], neg_half[0:TT, 0:NT], ALU.pow).then_inc(S[k + "_rstd"], 1)

            def low_part(g, k):
                wait(pool, S[k + "_hi"], g, 1, 1)
                q.tensor_tensor(xs[:, :, D:D + D2], xn[:, :, D1:D], xs[:, :, D1:D].bitcast(F32), ALU.subtract)
                q.tensor_tensor(xs[:, :, 2 * 128:3 * 128], xn[:, :, 0:D1], xs[:, :, 0:D1].bitcast(F32),
                                ALU.subtract).then_inc(S[k + "_lo"], 1)

            def residual_bias(g):
                wait(pool, S["hev"], g, 2, 2)
                wait(pool, S["h2s"], g, 2, 0)
                q.tensor_tensor(hb[:, :, :], h[:, :, :], bias_o[0:TT, :].unsqueeze(1).to_broadcast([TT, NT, D]),
                                ALU.add).then_inc(S["hbs"], 1)

            def router_pick(g):
                wait(pool, S["rprob"], g, 1, 1)
                wait(pool, S["comb"], g, CS, 0)
                p0, p1, p2 = (pr[:, :, e] for e in range(E))
                q.tensor_tensor(cmp[:, :, 0], p0, p1, ALU.subtract)
                q.tensor_tensor(cmp[:, :, 1], p0, p2, ALU.subtract)
                q.tensor_tensor(cmp[:, :, 2], p1, p2, ALU.subtract).then_inc(S["rcmp"], 1)
                wait_apart(pool, S["rcmp"], g, 4, 1, S["passed_p"])
                q.tensor_scalar(cmp[:, :, 0:3], cmp[:, :, 0:3], 0.0, None, ALU.is_ge).then_inc(S["rcmp"], 1)
                wait_apart(pool, S["rcmp"], g, 4, 2, S["passed_p"])
                q.tensor_scalar(cmp[:, :, 3:6], cmp[:, :, 0:3], -1.0, 1.0, ALU.mult, ALU.add).then_inc(S["rcmp"], 1)
                wait(pool, S["rcmp"], g, 4, 3)
                q.tensor_tensor(keep[:, :, 0], cmp[:, :, 3], cmp[:, :, 4], ALU.mult)
                q.tensor_tensor(keep[:, :, 1], cmp[:, :, 0], cmp[:, :, 5], ALU.mult)
                q.tensor_tensor(keep[:, :, 2], cmp[:, :, 1], cmp[:, :, 2], ALU.mult).then_inc(S["rcmp"], 1)
                wait_apart(pool, S["rcmp"], g, 4, 4, S["passed_p"])
                q.tensor_scalar(keep[:, :, :], keep[:, :, :], -1.0, 1.0, ALU.mult, ALU.add).then_inc(S["rkeep"], 1)
                wait(pool, S["rkeep"], g, 4, 1)
                q.tensor_tensor(keep[:, :, :], keep[:, :, :], pr[:, :, :], ALU.mult).then_inc(S["rkeep"], 1)
                wait(pool, S["rkeep"], g, 4, 2)
                q.tensor_tensor(den[:, :, 0], keep[:, :, 0], keep[:, :, 1], ALU.add).then_inc(S["rkeep"], 1)
                wait(pool, S["rkeep"], g, 4, 3)
                q.tensor_tensor(den[:, :, 1], den[:, :, 0], keep[:, :, 2], ALU.add).then_inc(S["rkeep"], 1)
                wait(pool, S["rden_s"], g, 1, 1)
                q.tensor_tensor(cw[:, :, :], keep[:, :, :], rden[:, :].unsqueeze(2).to_broadcast([TT, NT, E]),
                                ALU.mult).then_inc(S["cws"], 1)

            def split_low(k):
                pool.wait_ge(S["w_his"], k + 1)
                q.tensor_tensor(w_lo[:, :, PIECE * k:PIECE * (k + 1)], stage[:, k % 2, :, :],
                                w_hi[:, :, PIECE * k:PIECE * (k + 1)].bitcast(F32), ALU.subtract).then_inc(S["w_los_p"], 1)

            def step(g, ffn, nxt, nxt2, attn=True):
                if ffn:
                    router_pick(g + -1)
                if nxt:
                    ln_rstd(g + 1, "x")
                    low_part(g + 1, "x")
                if nxt2:
                    score_norm(g + 2)
                if attn:
                    ln_rstd(g, "y")
                if nxt:
                    residual_bias(g + 1)
                if attn:
                    low_part(g, "y")

            first = Group(None)
            score_norm(first)
            pool.wait_ge(S["ld_bias"], 32)
            ln_rstd(first, "x")
            low_part(first, "x")
            score_norm(first + 1)
            residual_bias(first)
            for k in range(NPQ, NPW):
                split_low(k)
            step(first, False, True, True)
            with pool.Fori(1, NG - 2) as i:
                step(Group(i), True, True, True)
            step(Group(None, NG - 2), True, True, False)
            step(Group(None, NG - 1), True, False, False)
            step(Group(None, NG), True, False, False, attn=False)


_INS = ['x', 'L0_tok_gamma', 'L0_tok_beta', 'L0_tok_w', 'L0_tok_b', 'L0_attn_w_qkv', 'L0_attn_w_out', 'L0_attn_b_out',
        'L0_ffn_shared_gate', 'L0_ffn_shared_up', 'L0_ffn_shared_down', 'L0_ffn_routed_gate', 'L0_ffn_routed_up',
        'L0_ffn_routed_down', 'L0_ffn_router_w', 'L0_ffn_routing_bias']
_OUTS = [((128, 87, 192), 'float32')]


def kernel(**inputs):
    import numpy as _np
    import concourse.bacc as _bacc
    from concourse import mybir as _mybir
    from concourse.bass_utils import run_bass_kernel_spmd as _run

    nc = _bacc.Bacc("TRN2", target_bir_lowering=False, num_devices=1)
    arrays, args = {}, []
    for name in _INS:
        a = _np.ascontiguousarray(inputs[name])
        arrays[f"in_{name}_dram"] = a
        args.append(nc.dram_tensor(f"in_{name}_dram", a.shape, _mybir.dt.from_np(a.dtype), kind="ExternalInput").ap())
    for i, (shape, dtype) in enumerate(_OUTS):
        dt = _mybir.dt.from_np(_np.dtype(dtype))
        args.append(nc.dram_tensor(f"out_{i}_dram", shape, dt, kind="ExternalOutput").ap())
    audio_tower_kernel(nc, *args)
    r = _run(nc, [arrays], core_ids=[0])
    return r.results[0]["out_0_dram"]
```

```python
from contextlib import ExitStack

import concourse.bass as bass
from concourse import mybir

ALU = mybir.AluOpType
ACT = mybir.ActivationFunctionType
F32 = mybir.dt.float32
F32R = mybir.dt.float32r
I16 = mybir.dt.int16
AX_X = mybir.AxisListType.X

LN_EPS = 1e-5
HEADS = 12
DH = 64
TOPK = 2


class Group:

    def __init__(self, reg, off=0):
        self.reg, self.off = reg, off

    def __add__(self, n):
        return Group(self.reg, self.off + n)

    def count(self, per, k):
        fixed = self.off * per + k
        return fixed if self.reg is None else self.reg * per + fixed

    def index(self):
        return self.count(1, 0)


def wait(eng, sem, g, per, k):
    v = g.count(per, k)
    if not isinstance(v, int) or v > 0:
        eng.wait_ge(sem, v)


def wait_apart(eng, sem, g, per, k, passed):
    wait(eng, sem, g, per, k)
    eng.sem_inc(passed, 1)


def audio_tower_kernel(nc, x, gamma, beta, tok_w, tok_b, w_qkv, w_out, b_out, sh_gate, sh_up, sh_down,
                       rt_gate, rt_up, rt_down, router_w, routing_bias, out):
    B, N, D = x.shape
    KEEP = int(N * 0.7)
    GB = 4
    NG = B // GB
    TOK = GB * KEEP
    NT = 3
    TT = TOK // NT
    D1 = 128
    D2 = D - D1
    INNER = HEADS * DH
    E = rt_gate.shape[0]
    NE = E + 1
    I = sh_gate.shape[1]
    IC = I // 128
    HC = NE * IC
    QK = 2 * INNER // 128
    OC = INNER // 128
    HU = 4
    UNITS = GB * HEADS // HU
    PH = HEADS // 2
    VH = INNER // 2
    VW = DH + 1
    NPR = QK + 2 * GB
    WC = 3 * INNER + NE * 2 * I
    PIECE = 768
    NPQ = 3 * INNER // PIECE
    NPW = WC // PIECE
    SCALE = DH ** -0.5
    assert TOK % NT == 0 and TOK <= 512 and NE * IC == UNITS and 2 * I == PIECE and E == 3 and TOPK == 2

    PAIRS = [(b, t) for b in range(GB) for t in range(NT)
             if b * KEEP < (t + 1) * TT and (b + 1) * KEEP > t * TT]
    NP = len(PAIRS)

    with ExitStack() as ctx:
        def sb(name, shape, dt=F32):
            return ctx.enter_context(nc.sbuf_tensor(name, shape, dt))

        def sem(name):
            return ctx.enter_context(nc.semaphore(name))

        w_hi = sb("w_hi", [128, 2, WC], F32R)
        w_lo = sb("w_lo", [128, 2, WC], F32R)
        w_down = sb("w_down", [128, NE, IC, D])
        w_o = sb("w_o", [128, OC, D])
        w_router = sb("w_router", [128, E, D])
        ident = sb("ident", [128, 128])
        earlier = sb("earlier", [N, N])
        place = sb("place", [N, NP, TT], I16)
        gw = sb("gw", [128, D])
        brow = sb("brow", [128, D])
        wrow = sb("wrow", [128, D])
        bias_o = sb("bias_o", [128, D])
        bias_r = sb("bias_r", [128, E])
        score0 = sb("score0", [128, 2])
        neg_half = sb("neg_half", [128, GB])
        eps = sb("eps", [128, GB])
        xt = sb("xt", [N, GB, D])
        xc = sb("xc", [N, GB, D])
        bst = sb("bst", [N, GB, 6])
        mv = sb("mv", [N, GB, 2])
        rstd = sb("rstd", [N, GB])
        neg_mean = sb("neg_mean", [N, GB])
        score = sb("score", [N, 3, GB])
        junk = sb("junk", [N, 2, N])
        rk = sb("rk", [N, 4, GB])
        mask = sb("mask", [N, NP, TT])
        h = sb("h", [TT, NT, D])
        hb = sb("hb", [TT, NT, D])
        h2 = sb("h2", [TT, NT, D])
        acc = sb("acc", [TT, NT, D])
        xn = sb("xn", [TT, NT, D])
        xs = sb("xs", [TT, NT, 3 * 128], F32R)
        lst = sb("lst", [TT, NT, 6])
        lmv = sb("lmv", [TT, NT, 2])
        lrs = sb("lrs", [TT, NT])
        xT = sb("xT", [128, 3, TOK], F32R)
        yT = sb("yT", [128, 3, TOK], F32R)
        qk = sb("qk", [128, QK, TOK])
        oT = qk[:, 0:OC, :]
        v1 = sb("v1", [KEEP, GB, HEADS, VW])
        def pairs_of(u):
            return [divmod(HU * (u // 2) + i, PH) for i in range(HU)]

        p = sb("p", [KEEP, 2, HU, KEEP])
        pT = sb("pT", [KEEP, 2, HU, KEEP])
        mx = sb("mx", [KEEP, 2, HU])
        rsum = sb("rsum", [KEEP, 2, HU])
        o = sb("o", [KEEP, GB * PH, 2 * DH])
        hT = sb("hT", [128, HC, TOK])
        th = sb("th", [128, 2, TOK])
        stage = hT[:, :, :].rearrange("p c n -> p (c n)")[:, 0:4 * PIECE].rearrange(
            "p (r a n) -> p r a n", r=2, a=2)
        z = sb("z", [TT, NT, E])
        rjunk = sb("rjunk", [TT, E, D])
        ez = sb("ez", [TT, NT, E])
        pr = sb("pr", [TT, NT, E])
        cmp = sb("cmp", [TT, NT, 6])
        keep = sb("keep", [TT, NT, E])
        den = sb("den", [TT, NT, 2])
        rden = sb("rden", [TT, NT])
        cw = sb("cw", [TT, NT, E])

        ps = ctx.enter_context(nc.psum_tensor("ps", [128, 8, 512], F32))
        GU0 = 4

        names = """ld_const ld_bias ld_w0 ld_w1 ld_x st_out ld_small
            c_ident c_mask c_ones c_neg c_gw c_bw c_s0 c_rw w_his w_los_d w_los_p
            f_bn f_aggr f_negmu f_eps f_rstd f_xc f_dot f_scale f_score f_bc f_rank f_rk f_mask
            sel hev hbs
            x_bn x_aggr x_eps x_rstd x_norm x_hi x_lo
            y_bn y_aggr y_eps y_rstd y_norm y_hi y_lo
            xt_pe xev_a xev_d prj prj_a prj_d
            s_pe smax ssub sexp t_pe pte pv_pe orec onm ot_pe oev_a oev_d wo_pe h2s
            yt_pe yev_a yev_d gate_pe up_pe tanhs silus hts dn_pe comb
            passed_d passed_p
            rdot rz rexp rone rprob rcmp rkeep rden_s cws""".split()
        S = {n: sem("s_" + n) for n in names}

        def bank(k, parts, cols):
            return ps[0:parts, k, 0:cols]

        DVE_OUT = [n for n in range(NPR) if n % 4 == 3]
        ACT_OUT = [n for n in range(NPR) if n % 4 != 3]

        def copied(eng, g, n):
            d, a = sum(m <= n for m in DVE_OUT), sum(m <= n for m in ACT_OUT)
            wait(eng, S["prj_a"], g, len(ACT_OUT), a)
            wait(eng, S["prj_d"], g, len(DVE_OUT), d)

        TERMS = [("lo", 0, 0), ("hi", 0, 2), ("lo", 1, 1), ("hi", 1, 1), ("hi", 0, 0)]
        half = {"hi": w_hi, "lo": w_lo}
        CS = 4 * NT

        block = ctx.enter_context(nc.Block())

        @block.sync
        def _(sp):
            def bcast(dst, src, done):
                sp.dma_start(dst[:, :], src.partition_broadcast(128)).then_inc(S[done], 16)

            def load_x(g):
                v = g.index()
                src = x[v * GB:v * GB + GB] if isinstance(v, int) else x[bass.ds(v * GB, GB), :, :]
                sp.dma_start(xt[:, :, :], src.rearrange("b n d -> n b d")).then_inc(S["ld_x"], 16)

            def load_piece(k):
                if k >= 2:
                    if k - 2 < NPQ:
                        sp.wait_ge(S["w_los_d"], k - 1)
                    else:
                        sp.wait_ge(S["w_los_p"], k - 1 - NPQ)
                if k < NPQ:
                    parts = [(w_qkv[:, PIECE * k:PIECE * (k + 1)], 0, PIECE)]
                else:
                    e = k - NPQ
                    gt, up = (sh_gate, sh_up) if e == 0 else (rt_gate[e - 1], rt_up[e - 1])
                    parts = [(gt, 0, I), (up, I, 2 * I)]
                for w, a, b in parts:
                    sp.dma_start(stage[:, k % 2, 0, a:b], w[0:D1, :]).then_inc(S[f"ld_w{k % 2}"], 16)
                    sp.dma_start(stage[0:D2, k % 2, 1, a:b], w[D1:D, :]).then_inc(S[f"ld_w{k % 2}"], 16)
                    sp.dma_start(stage[D2:2 * D2, k % 2, 1, a:b], w[D1:D, :]).then_inc(S[f"ld_w{k % 2}"], 16)

            def store(g):
                sp.wait_ge(S["comb"], g.count(CS, CS))
                v = g.index()
                flat = out.rearrange("b k d -> (b k) d")
                dst = flat[v * TOK:(v + 1) * TOK] if isinstance(v, int) else flat[bass.ds(v * TOK, TOK), :]
                sp.dma_start(dst.rearrange("(t q) d -> q t d", t=NT), acc[:, :, :]).then_inc(S["st_out"], 16)

            load_x(Group(None))
            bcast(gw, gamma, "ld_const")
            bcast(wrow, tok_w, "ld_const")
            bcast(brow, beta, "ld_const")
            sp.dma_start(score0[:, 1:2], tok_b.partition_broadcast(128)).then_inc(S["ld_const"], 16)
            load_piece(0)
            load_piece(1)
            bcast(bias_o, b_out, "ld_bias")
            bcast(bias_r, routing_bias, "ld_bias")
            sp.dma_start(rjunk[:, :, :].rearrange("q e d -> q (e d)"),
                         router_w.rearrange("d e -> (d e)").partition_broadcast(TT)).then_inc(S["ld_bias"], 16)
            for k in range(2, NPQ):
                load_piece(k)
            sp.dma_start(w_o[:, :, :], w_out.rearrange("(c p) d -> p c d", p=128)).then_inc(S["ld_small"], 16)
            sp.dma_start(w_down[:, 0, :, :], sh_down.rearrange("(c p) d -> p c d", p=128)).then_inc(S["ld_small"], 16)
            for e in range(E):
                sp.dma_start(w_down[:, e + 1, :, :],
                             rt_down[e].rearrange("(c p) d -> p c d", p=128)).then_inc(S["ld_small"], 16)
            sp.wait_ge(S["sel"], 2)
            load_x(Group(None, 1))
            for k in range(NPQ, NPW):
                load_piece(k)

            def step(g, ffn, nxt, nxt2):
                if nxt2:
                    wait(sp, S["sel"], g + 1, 2, 2)
                    load_x(g + 2)
                if ffn:
                    store(g + -1)

            step(Group(None), False, True, True)
            with sp.Fori(1, NG - 2) as i:
                step(Group(i), True, True, True)
            step(Group(None, NG - 2), True, True, False)
            step(Group(None, NG - 1), True, False, False)
            store(Group(None, NG - 1))
            sp.wait_ge(S["st_out"], 16 * NG)

        @block.tensor
        def _(pe):
            mm = nc.tensor.matmul

            def rank_rows(g):
                wait(pe, S["f_score"], g, 1, 1)
                wait(pe, S["xev_d"], g + -1, 1, 1)
                for b in range(GB):
                    last = mm(ps[0:N, 3, b * N:(b + 1) * N], score[:, 2, b:b + 1].to_broadcast([N, N]),
                              ident[0:N, 0:N], start=True, stop=True, is_transpose=True)
                last.then_inc(S["f_bc"], 1)

            def select(g, tiles):
                if 0 in tiles:
                    wait(pe, S["f_mask"], g, GB, GB)
                    wait(pe, S["ld_x"], g, 16, 16)
                    wait(pe, S["pte"], g, UNITS, 0)
                for t in tiles:
                    if t == NT - 1:
                        wait(pe, S["onm"], g, UNITS, 0)
                    mine = [n for n, (b, u) in enumerate(PAIRS) if u == t]
                    dst = ps[0:TT, 2, t * D:(t + 1) * D] if t < NT - 1 else ps[0:TT, 3, 0:D]
                    for n in mine:
                        last = mm(dst, mask[:, n, :], xt[:, PAIRS[n][0], :], start=(n == mine[0]), stop=(n == mine[-1]))
                    if t >= NT - 2:
                        last.then_inc(S["sel"], 1)

            def to_features(banks, done):
                for k in range(3):
                    for t in range(NT):
                        last = mm(ps[:, banks[k], t * TT:(t + 1) * TT], xs[:, t, 128 * k:128 * (k + 1)].bitcast(F32),
                                  ident[0:TT, 0:TT], start=True, stop=True, is_transpose=True)
                    last.then_inc(done, 1)

            def tokens_to_features(g):
                wait(pe, S["x_hi"], g, 1, 1)
                wait(pe, S["x_lo"], g, 1, 1)
                wait(pe, S["oev_a"], g, OC // 2, 0)
                to_features((2, 3, 0), S["xt_pe"])

            def project(g, rows, experts):
                wait(pe, S["xev_a"], g, 2, 2)
                wait(pe, S["xev_d"], g, 1, 1)
                for n in range(NPR):
                    bk = GU0 + n % 4
                    if n < 4:
                        wait(pe, S["comb"], g + -2, CS, CS)
                    else:
                        m = n - 4
                        if m in DVE_OUT:
                            wait(pe, S["prj_d"], g, len(DVE_OUT), DVE_OUT.index(m) + 1)
                        else:
                            wait(pe, S["prj_a"], g, len(ACT_OUT), ACT_OUT.index(m) + 1)
                    if g.reg is None and g.off == 0:
                        k = min(n * 128 // PIECE, NPQ - 1)
                        if n in (0, PIECE // 128, QK):
                            pe.wait_ge(S["w_his"], k + 1)
                            pe.wait_ge(S["w_los_d"], k + 1)
                    if n < QK:
                        dst = bank(bk, 128, TOK)
                    else:
                        b, f = divmod(n - QK, 2)
                        dst = bank(bk, KEEP, VH)
                    for k, (hl, wc, xk) in enumerate(TERMS):
                        w = half[hl]
                        if n < QK:
                            last = mm(dst, w[:, wc, 128 * n:128 * (n + 1)], xT[:, xk, :], start=(k == 0), stop=(k == 4))
                        else:
                            c0 = 2 * INNER + VH * f
                            last = mm(dst, xT[:, xk, KEEP * b:KEEP * (b + 1)], w[:, wc, c0:c0 + VH],
                                      start=(k == 0), stop=(k == 4))
                    last.then_inc(S["prj"], 1)
                    if n == 6 and rows is not None:
                        rank_rows(rows)
                    if n == 15 and experts is not None:
                        experts_to_features(experts)

            def scores(g, u):
                if u == 0:
                    copied(pe, g, QK - 1)
                    wait(pe, S["yev_d"], g + -1, 1, 1)
                    wait(pe, S["yev_a"], g + -1, 2, 2)
                if u >= 2:
                    wait(pe, S["ssub"], g, UNITS, u - 1)
                r = DH * (u % 2)
                for i, (b, c) in enumerate(pairs_of(u)):
                    last = mm(ps[0:KEEP, u % 2, i * KEEP:(i + 1) * KEEP], qk[r:r + DH, c, KEEP * b:KEEP * (b + 1)],
                              qk[r:r + DH, QK // 2 + c, KEEP * b:KEEP * (b + 1)], start=True, stop=True)
                last.then_inc(S["s_pe"], 1)

            def transpose_p(g, u):
                wait(pe, S["sexp"], g, UNITS, u + 1)
                if u > 0:
                    wait(pe, S["pte"], g, UNITS, u)
                for k in range(HU):
                    last = mm(ps[0:KEEP, 2, k * KEEP:(k + 1) * KEEP], p[:, u % 2, k, :], ident[0:KEEP, 0:KEEP],
                              start=True, stop=True, is_transpose=True)
                last.then_inc(S["t_pe"], 1)

            def weigh_v(g, u, ranked=False):
                wait(pe, S["pte"], g, UNITS, u + 1)
                if u == 0:
                    copied(pe, g, NPR - 1)
                if u == 0 and ranked:
                    wait(pe, S["f_rank"], g + 1, 2 * GB, 2 * GB)
                if u > 0:
                    wait(pe, S["onm"], g, UNITS, u)
                for i, (b, c) in enumerate(pairs_of(u)):
                    last = mm(ps[0:KEEP, 3, i * VW:(i + 1) * VW], pT[:, u % 2, i, :], v1[:, b, 2 * c + u % 2, :],
                              start=True, stop=True)
                last.then_inc(S["pv_pe"], 1)

            def gate_up(g, c, projected):
                if c == 0:
                    wait(pe, S["yev_a"], g, 2, 2)
                    wait(pe, S["yev_d"], g, 1, 1)
                    if g.reg is None and g.off == 0:
                        pe.wait_ge(S["w_his"], NPW)
                        pe.wait_ge(S["w_los_p"], NPW - NPQ)
                if c == 0 and projected:
                    copied(pe, g + 1, NPR - 1)
                if c == 0 and not projected:
                    wait(pe, S["comb"], g, CS, 0)
                if c >= 2:
                    wait(pe, S["hts"], g, HC, c - 1)
                e, ic = divmod(c, IC)
                for up in range(2):
                    dst = bank(GU0 + 2 * (c % 2) + up, 128, TOK)
                    c0 = 3 * INNER + e * 2 * I + up * I + 128 * ic
                    for k, (hl, wc, xk) in enumerate(TERMS):
                        last = mm(dst, half[hl][:, wc, c0:c0 + 128], yT[:, xk, :], start=(k == 0), stop=(k == 4))
                    last.then_inc(S["up_pe" if up else "gate_pe"], 1)

            def down(g, n):
                t, pair = divmod(n, 2)
                if n == 0:
                    wait(pe, S["hts"], g, HC, HC)
                    if g.reg is None and g.off == 0:
                        pe.wait_ge(S["ld_small"], 16 * (1 + NE))
                if n >= 4:
                    wait(pe, S["comb"], g, CS, 2 * (n - 3))
                for e in range(2):
                    for c in range(IC):
                        ex = 2 * pair + e
                        last = mm(ps[0:TT, GU0 + n % 4, D * e:D * (e + 1)], hT[:, ex * IC + c, TT * t:TT * (t + 1)],
                                  w_down[:, ex, c, :], start=(c == 0), stop=(c == IC - 1))
                last.then_inc(S["dn_pe"], 1)

            def out_to_features(g, c):
                if c == 0:
                    wait(pe, S["onm"], g, UNITS, UNITS)
                    wait(pe, S["ssub"], g, UNITS, UNITS)
                if c >= 2:
                    wait(pe, S["oev_a" if c % 2 == 0 else "oev_d"], g, OC // 2, c // 2)
                for b in range(GB):
                    last = mm(ps[:, c % 2, KEEP * b:KEEP * (b + 1)], o[:, b * PH + c, :],
                              ident[0:KEEP, 0:KEEP], start=True, stop=True, is_transpose=True)
                last.then_inc(S["ot_pe"], 1)

            def project_out(g, nxt):
                wait(pe, S["oev_a"], g, OC // 2, OC // 2)
                wait(pe, S["oev_d"], g, OC // 2, OC // 2)
                if nxt:
                    wait(pe, S["xev_a"], g + 1, 2, 1)
                if g.reg is None and g.off == 0:
                    pe.wait_ge(S["ld_small"], 16 * (1 + NE))
                for t in range(NT):
                    dst = ps[0:TT, 1, t * D:(t + 1) * D] if t < NT - 1 else ps[0:TT, 2, 0:D]
                    for c in range(OC):
                        last = mm(dst, oT[:, c, TT * t:TT * (t + 1)], w_o[:, c, :], start=(c == 0), stop=(c == OC - 1))
                    if t >= NT - 2:
                        last.then_inc(S["wo_pe"], 1)

            def experts_to_features(g):
                wait(pe, S["y_hi"], g, 1, 1)
                wait(pe, S["y_lo"], g, 1, 1)
                to_features((2, 0, 1), S["yt_pe"])

            def step(g, ffn, nxt, nxt2, attn=True):
                for s in range(UNITS + 1):
                    if attn and s < UNITS:
                        scores(g, s)
                    if ffn and s >= 1:
                        gate_up(g + -1, s - 1, attn)
                    if attn and s >= 1:
                        transpose_p(g, s - 1)
                    if attn and s >= 2:
                        weigh_v(g, s - 2, nxt)
                if nxt:
                    select(g + 1, range(NT - 1))
                if attn:
                    weigh_v(g, UNITS - 1)
                if ffn:
                    down(g + -1, 0)
                if nxt:
                    select(g + 1, [NT - 1])
                for c in range(OC):
                    if attn:
                        out_to_features(g, c)
                    if ffn and c + 1 < 2 * NT:
                        down(g + -1, c + 1)
                if nxt:
                    tokens_to_features(g + 1)
                if attn:
                    project_out(g, nxt)
                if nxt:
                    project(g + 1, g + 2 if nxt2 else None, g)
                elif attn:
                    experts_to_features(g)

            pe.wait_ge(S["c_ident"], 2)
            first = Group(None)
            rank_rows(first)
            select(first, range(NT))
            tokens_to_features(first)
            project(first, first + 1, None)
            step(first, False, True, True)
            with pe.Fori(1, NG - 2) as i:
                step(Group(i), True, True, True)
            step(Group(None, NG - 2), True, True, False)
            step(Group(None, NG - 1), True, False, False)
            step(Group(None, NG), True, False, False, attn=False)

        @block.scalar
        def _(act):
            af = nc.scalar.activation

            def split_weights(k):
                loads = sum(3 if m < NPQ else 6 for m in range(k % 2, k + 1, 2))
                act.wait_ge(S[f"ld_w{k % 2}"], 16 * loads)
                af(w_hi[:, :, PIECE * k:PIECE * (k + 1)], stage[:, k % 2, :, :], ACT.Copy).then_inc(S["w_his"], 1)

            def copy_selected(g):
                wait(act, S["sel"], g, 2, 1)
                wait(act, S["hbs"], g, 1, 0)
                af(h[:, 0:2, :], ps[0:TT, 2, 0:2 * D].rearrange("q (t d) -> q t d", t=2), ACT.Copy).then_inc(S["hev"], 1)
                wait(act, S["sel"], g, 2, 2)
                af(h[:, 2, :], ps[0:TT, 3, 0:D], ACT.Copy).then_inc(S["hev"], 1)

            def high_part_tokens(g):
                wait(act, S["x_norm"], g, 1, 1)
                wait(act, S["yt_pe"], g + -1, 3, 0)
                af(xs[:, :, 0:D], xn[:, :, :], ACT.Copy).then_inc(S["x_hi"], 1)

            def high_part_experts(g, nxt):
                wait(act, S["y_norm"], g, 1, 1)
                if nxt:
                    wait(act, S["xt_pe"], g + 1, 3, 3)
                af(xs[:, :, 0:D], xn[:, :, :], ACT.Copy).then_inc(S["y_hi"], 1)

            def centre(g):
                wait(act, S["f_negmu"], g, 1, 1)
                wait(act, S["f_dot"], g, GB, 0)
                for b in range(GB):
                    af(xc[:, b, :], xt[:, b, :], ACT.Identity, bias=neg_mean[:, b:b + 1]).then_inc(S["f_xc"], 1)

            def features(dst, k, bk, src, g, done):
                wait(act, src, g, 3, k + 1)
                af(dst[:, k, :], bank(bk, 128, TOK), ACT.Copy).then_inc(done, 1)

            def projected(g, n):
                wait(act, S["prj"], g, NPR, n + 1)
                if n < QK:
                    af(qk[:, n, :], bank(GU0 + n % 4, 128, TOK), ACT.Copy).then_inc(S["prj_a"], 1)
                else:
                    b, f = divmod(n - QK, 2)
                    af(v1[:, b, f * 6:f * 6 + 6, 0:DH],
                       bank(GU0 + n % 4, KEEP, VH).rearrange("q (a d) -> q a d", d=DH), ACT.Copy).then_inc(S["prj_a"], 1)

            def exponentials(g, u):
                wait(act, S["ssub"], g, UNITS, u + 1)
                v = p[:, u % 2, :, :]
                af(v, v, ACT.Exp, scale=SCALE).then_inc(S["sexp"], 1)

            def copy_pT(g, u):
                wait(act, S["t_pe"], g, UNITS, u + 1)
                if u >= 2:
                    wait(act, S["pv_pe"], g, UNITS, u - 1)
                af(pT[:, u % 2, :, :], bank(2, KEEP, HU * KEEP).rearrange("q (a n) -> q a n", a=HU),
                   ACT.Copy).then_inc(S["pte"], 1)

            def tanh_gate(g, c):
                wait(act, S["gate_pe"], g, HC, c + 1)
                if c >= 2:
                    wait(act, S["hts"], g, HC, c - 1)
                af(th[:, c % 2, :], bank(GU0 + 2 * (c % 2), 128, TOK), ACT.Tanh, scale=0.5).then_inc(S["tanhs"], 1)

            def out_features(g, c):
                wait(act, S["ot_pe"], g, OC, c + 1)
                af(oT[:, c, :], bank(c % 2, 128, TOK), ACT.Copy).then_inc(S["oev_a"], 1)

            def router_exp(g):
                wait(act, S["rz"], g, 1, 1)
                af(ez[:, :, :], z[:, :, :], ACT.Exp, scale=-1.0).then_inc(S["rexp"], 1)

            def step(g, ffn, nxt, nxt2, attn=True):
                for s in range(UNITS + 1):
                    if ffn and s >= 1:
                        tanh_gate(g + -1, s - 1)
                    if attn and s < UNITS:
                        exponentials(g, s)
                    if attn and s >= 1:
                        copy_pT(g, s - 1)
                if nxt:
                    copy_selected(g + 1)
                if attn:
                    out_features(g, 0)
                    out_features(g, 2)
                if nxt:
                    high_part_tokens(g + 1)
                if attn:
                    out_features(g, 4)
                if nxt:
                    features(xT, 0, 2, S["xt_pe"], g + 1, S["xev_a"])
                    features(xT, 2, 0, S["xt_pe"], g + 1, S["xev_a"])
                if nxt2:
                    centre(g + 2)
                if nxt:
                    for n in ACT_OUT[0:5]:
                        projected(g + 1, n)
                if attn:
                    high_part_experts(g, nxt)
                if nxt:
                    for n in ACT_OUT[5:12]:
                        projected(g + 1, n)
                if attn:
                    features(yT, 0, 2, S["yt_pe"], g, S["yev_a"])
                    features(yT, 2, 1, S["yt_pe"], g, S["yev_a"])
                if nxt:
                    for n in ACT_OUT[12:]:
                        projected(g + 1, n)
                if attn:
                    router_exp(g)

            first = Group(None)
            split_weights(0)
            centre(first)
            for k in range(1, NPQ):
                split_weights(k)
            copy_selected(first)
            high_part_tokens(first)
            centre(first + 1)
            features(xT, 0, 2, S["xt_pe"], first, S["xev_a"])
            features(xT, 2, 0, S["xt_pe"], first, S["xev_a"])
            for n in ACT_OUT:
                projected(first, n)
            for k in range(NPQ, NPW):
                split_weights(k)
            step(first, False, True, True)
            with act.Fori(1, NG - 2) as i:
                step(Group(i), True, True, True)
            step(Group(None, NG - 2), True, True, False)
            step(Group(None, NG - 1), True, False, False)
            step(Group(None, NG), True, False, False, attn=False)

        @block.vector
        def _(dve):
            v = nc.vector

            def split_low(k):
                dve.wait_ge(S["w_his"], k + 1)
                v.tensor_tensor(w_lo[:, :, PIECE * k:PIECE * (k + 1)], stage[:, k % 2, :, :],
                                w_hi[:, :, PIECE * k:PIECE * (k + 1)].bitcast(F32), ALU.subtract).then_inc(S["w_los_d"], 1)

            def score_stats(g):
                wait(dve, S["ld_x"], g, 16, 16)
                for b in range(GB):
                    v.bn_stats(bst[:, b, :], xt[:, b, :]).then_inc(S["f_bn"], 1)
                wait(dve, S["f_bn"], g, GB, GB)
                wait_apart(dve, S["f_eps"], g, 1, 0, S["passed_d"])
                for b in range(GB):
                    v.bn_aggr(mv[:, b, :], bst[:, b, :]).then_inc(S["f_aggr"], 1)
                wait(dve, S["f_aggr"], g, GB, GB)
                wait(dve, S["f_xc"], g, GB, 0)
                v.tensor_scalar(neg_mean[:, :], mv[:, :, 0], -1.0, None, ALU.mult).then_inc(S["f_negmu"], 1)

            def score_dots(g):
                for b in range(GB):
                    wait(dve, S["f_xc"], g, GB, b + 1)
                    v.tensor_tensor_reduce(out=xc[:, b, :], in0=xc[:, b, :], in1=gw[0:N, :], scale=1.0, scalar=0.0,
                                           op0=ALU.mult, op1=ALU.add, accum_out=score[:, 0, b:b + 1]).then_inc(S["f_dot"], 1)
                wait(dve, S["f_dot"], g, GB, GB)
                wait(dve, S["f_rstd"], g, 1, 1)
                v.tensor_tensor(score[:, 1, :], score[:, 0, :], rstd[:, :], ALU.mult).then_inc(S["f_scale"], 1)
                wait(dve, S["f_scale"], g, 1, 1)
                v.tensor_scalar(score[:, 2, :], score[:, 1, :], score0[0:N, 0:1], None, ALU.add).then_inc(S["f_score"], 1)

            def rank(g, b):
                wait(dve, S["f_bc"], g, 1, 1)
                row = ps[0:N, 3, b * N:(b + 1) * N]
                s = score[:, 2, b:b + 1]
                wait(dve, S["f_rank"], g, 2 * GB, 2 * b - 1)
                v.tensor_scalar(junk[:, 0, :], row, s, None, ALU.is_gt, ALU.add,
                                accum_out=rk[:, 0, b:b + 1]).then_inc(S["f_rank"], 1)
                wait(dve, S["f_rank"], g, 2 * GB, 2 * b)
                v.scalar_tensor_tensor(out=junk[:, 1, :], in0=row, scalar=s, in1=earlier[:, :], op0=ALU.is_equal,
                                       op1=ALU.mult, accum_out=rk[:, 1, b:b + 1]).then_inc(S["f_rank"], 1)

            def masks(g):
                wait(dve, S["f_rank"], g, 2 * GB, 2 * GB)
                v.tensor_tensor(rk[:, 2, :], rk[:, 0, :], rk[:, 1, :], ALU.add).then_inc(S["f_rk"], 1)
                wait(dve, S["f_rk"], g, 3, 1)
                v.tensor_scalar(rk[:, 3, :], rk[:, 2, :], float(KEEP), 4096.0, ALU.is_ge, ALU.mult).then_inc(S["f_rk"], 1)
                wait(dve, S["f_rk"], g, 3, 2)
                v.tensor_tensor(rk[:, 3, :], rk[:, 3, :], rk[:, 2, :], ALU.add).then_inc(S["f_rk"], 1)
                wait(dve, S["f_rk"], g, 3, 3)
                wait(dve, S["sel"], g, 2, 0)
                for b in range(GB):
                    mine = [n for n, (c, t) in enumerate(PAIRS) if c == b]
                    a, z_ = mine[0], mine[-1] + 1
                    v.tensor_scalar(mask[:, a:z_, :], place[:, a:z_, :], rk[:, 3, b:b + 1], None,
                                    ALU.is_equal).then_inc(S["f_mask"], 1)

            def ln_stats(src, g, k):
                for t in range(NT):
                    v.bn_stats(lst[:, t, :], src[:, t, :]).then_inc(S[k + "_bn"], 1)
                wait_apart(dve, S[k + "_bn"], g, NT, NT, S["passed_d"])
                for t in range(NT):
                    v.bn_aggr(lmv[:, t, :], lst[:, t, :]).then_inc(S[k + "_aggr"], 1)

            def normalise(src, g, k, other, split):
                wait(dve, S[k + "_rstd"], g, 1, 1)
                wait(dve, S[other + "_hi"], split, 1, 1)
                wait(dve, S[other + "_lo"], split, 1, 1)
                for t in range(NT):
                    last = v.tensor_scalar(xn[:, t, :], src[:, t, :], lmv[:, t, 0:1], lrs[:, t:t + 1],
                                           ALU.subtract, ALU.mult)
                last.then_inc(S[k + "_norm"], 1)

            def features(dst, bk, src, g, done):
                wait(dve, src, g, 3, 2)
                v.tensor_copy(dst[:, 1, :], bank(bk, 128, TOK)).then_inc(done, 1)

            def projected(g, n):
                wait(dve, S["prj"], g, NPR, n + 1)
                if n < QK:
                    v.tensor_copy(qk[:, n, :], bank(GU0 + n % 4, 128, TOK)).then_inc(S["prj_d"], 1)
                else:
                    b, f = divmod(n - QK, 2)
                    v.tensor_copy(v1[:, b, f * 6:f * 6 + 6, 0:DH],
                                  bank(GU0 + n % 4, KEEP, VH).rearrange("q (a d) -> q a d", d=DH)).then_inc(S["prj_d"], 1)

            def row_max(g, u):
                wait(dve, S["s_pe"], g, UNITS, u + 1)
                v.tensor_reduce(mx[:, u % 2, :], bank(u % 2, KEEP, HU * KEEP).rearrange("q (a m) -> q a m", a=HU),
                                AX_X, ALU.max).then_inc(S["smax"], 1)

            def shift_scores(g, u):
                wait(dve, S["smax"], g, UNITS, u + 1)
                if u >= 2:
                    wait(dve, S["t_pe"], g, UNITS, u - 1)
                v.tensor_tensor(p[:, u % 2, :, :], bank(u % 2, KEEP, HU * KEEP).rearrange("q (a m) -> q a m", a=HU),
                                mx[:, u % 2, :].unsqueeze(2).to_broadcast([KEEP, HU, KEEP]),
                                ALU.subtract).then_inc(S["ssub"], 1)

            def row_sums(g, u):
                wait(dve, S["pv_pe"], g, UNITS, u + 1)
                s = bank(3, KEEP, HU * VW).rearrange("q (a d) -> q a d", a=HU)
                v.reciprocal(rsum[:, u % 2, :], s[:, :, DH]).then_inc(S["orec"], 1)

            def normalise_out(g, u):
                s = bank(3, KEEP, HU * VW).rearrange("q (a d) -> q a d", a=HU)
                wait(dve, S["orec"], g, UNITS, u + 1)
                if u == 0:
                    wait(dve, S["ot_pe"], g, OC, 0)
                k = HU * (u // 2)
                v.tensor_tensor(o[:, k:k + HU, DH * (u % 2):DH * (u % 2 + 1)], s[:, :, 0:DH],
                                rsum[:, u % 2, :].unsqueeze(2).to_broadcast([KEEP, HU, DH]),
                                ALU.mult).then_inc(S["onm"], 1)

            def gated(g, c):
                wait(dve, S["tanhs"], g, HC, c + 1)
                t = th[:, c % 2, :]
                v.scalar_tensor_tensor(out=t, in0=t, scalar=1.0, in1=bank(GU0 + 2 * (c % 2), 128, TOK), op0=ALU.add,
                                       op1=ALU.mult).then_inc(S["silus"], 1)

            def hidden(g, c):
                wait(dve, S["silus"], g, HC, c + 1)
                wait(dve, S["up_pe"], g, HC, c + 1)
                v.scalar_tensor_tensor(out=hT[:, c, :], in0=th[:, c % 2, :], scalar=0.5,
                                       in1=bank(GU0 + 2 * (c % 2) + 1, 128, TOK),
                                       op0=ALU.mult, op1=ALU.mult).then_inc(S["hts"], 1)

            def out_features(g, c):
                wait(dve, S["ot_pe"], g, OC, c + 1)
                v.tensor_copy(oT[:, c, :], bank(c % 2, 128, TOK)).then_inc(S["oev_d"], 1)

            def combine(g, n):
                t, pair = divmod(n, 2)
                if n == 0:
                    wait(dve, S["cws"], g, 1, 1)
                    wait(dve, S["st_out"], g, 16, 0)
                wait(dve, S["dn_pe"], g, 2 * NT, n + 1)
                bk = ps[0:TT, GU0 + n % 4, :]
                a = acc[:, t, :]

                def mine(k):
                    wait(dve, S["comb"], g, CS, 4 * t + k)
                if pair == 0:
                    v.tensor_tensor(a, bk[:, 0:D], h2[:, t, :], ALU.add).then_inc(S["comb"], 1)
                    mine(1)
                    v.scalar_tensor_tensor(out=a, in0=bk[:, D:2 * D], scalar=cw[:, t, 0:1], in1=a, op0=ALU.mult,
                                           op1=ALU.add).then_inc(S["comb"], 1)
                else:
                    mine(2)
                    v.scalar_tensor_tensor(out=a, in0=bk[:, 0:D], scalar=cw[:, t, 1:2], in1=a, op0=ALU.mult,
                                           op1=ALU.add).then_inc(S["comb"], 1)
                    mine(3)
                    v.scalar_tensor_tensor(out=a, in0=bk[:, D:2 * D], scalar=cw[:, t, 2:3], in1=a, op0=ALU.mult,
                                           op1=ALU.add).then_inc(S["comb"], 1)

            def residual(g):
                wait(dve, S["hbs"], g, 1, 1)
                wait(dve, S["wo_pe"], g, 2, 1)
                v.tensor_tensor(h2[:, 0:2, :], ps[0:TT, 1, 0:2 * D].rearrange("q (t d) -> q t d", t=2), hb[:, 0:2, :],
                                ALU.add).then_inc(S["h2s"], 1)
                wait(dve, S["wo_pe"], g, 2, 2)
                v.tensor_tensor(h2[:, 2, :], ps[0:TT, 2, 0:D], hb[:, 2, :], ALU.add).then_inc(S["h2s"], 1)
                wait(dve, S["h2s"], g, 2, 2)

            def router_dots(g, t):
                if t == 0:
                    wait(dve, S["y_norm"], g, 1, 1)
                for e in range(E):
                    n = t * E + e
                    wait(dve, S["rdot"], g, E * NT, n - E + 1)
                    v.tensor_tensor_reduce(out=rjunk[:, e, :], in0=xn[:, t, :], in1=w_router[0:TT, e, :], scale=1.0,
                                           scalar=0.0, op0=ALU.mult, op1=ALU.add,
                                           accum_out=z[:, t, e:e + 1]).then_inc(S["rdot"], 1)

            def router_logits(g):
                wait(dve, S["rdot"], g, E * NT, E * NT)
                v.tensor_tensor(z[:, :, :], z[:, :, :], bias_r[0:TT, :].unsqueeze(1).to_broadcast([TT, NT, E]),
                                ALU.add).then_inc(S["rz"], 1)

            def router_probs(g):
                wait(dve, S["rexp"], g, 1, 1)
                v.tensor_scalar(ez[:, :, :], ez[:, :, :], 1.0, None, ALU.add).then_inc(S["rone"], 1)
                wait(dve, S["rone"], g, 1, 1)
                v.reciprocal(pr[:, :, :], ez[:, :, :]).then_inc(S["rprob"], 1)

            def router_share(g):
                wait(dve, S["rkeep"], g, 4, 4)
                v.reciprocal(rden[:, :], den[:, :, 1]).then_inc(S["rden_s"], 1)

            def step(g, ffn, nxt, nxt2, attn=True):
                for s in range(UNITS + 1):
                    if attn and s == 1 and (g.reg is not None or g.off > 0):
                        router_probs(g + -1)
                    if attn and s == 4 and (g.reg is not None or g.off > 0):
                        router_share(g + -1)
                    if not attn and s == 0:
                        router_probs(g + -1)
                        router_share(g + -1)
                    if attn and s >= 3:
                        row_sums(g, s - 3)
                    if ffn and s >= 2:
                        gated(g + -1, s - 2)
                    if attn and s >= 3:
                        normalise_out(g, s - 3)
                    if attn and s < UNITS:
                        row_max(g, s)
                    if ffn and s >= 2:
                        hidden(g + -1, s - 2)
                    if attn and s < UNITS:
                        shift_scores(g, s)
                if attn:
                    row_sums(g, UNITS - 2)
                if ffn:
                    gated(g + -1, HC - 1)
                if attn:
                    normalise_out(g, UNITS - 2)
                if ffn:
                    hidden(g + -1, HC - 1)
                if attn:
                    row_sums(g, UNITS - 1)
                    normalise_out(g, UNITS - 1)
                if ffn:
                    combine(g + -1, 0)
                if nxt:
                    wait(dve, S["hev"], g + 1, 2, 2)
                    ln_stats(h, g + 1, "x")
                if attn:
                    out_features(g, 1)
                if ffn:
                    combine(g + -1, 1)
                if nxt:
                    normalise(h, g + 1, "x", "y", g + -1)
                if ffn:
                    combine(g + -1, 2)
                if attn:
                    out_features(g, 3)
                if ffn:
                    combine(g + -1, 3)
                if nxt2:
                    score_stats(g + 2)
                if ffn:
                    combine(g + -1, 4)
                if attn:
                    out_features(g, 5)
                if nxt:
                    features(xT, 3, S["xt_pe"], g + 1, S["xev_d"])
                if ffn:
                    combine(g + -1, 5)
                if nxt2:
                    score_dots(g + 2)
                if attn:
                    residual(g)
                    ln_stats(h2, g, "y")
                if nxt:
                    projected(g + 1, 3)
                if attn:
                    normalise(h2, g, "y", "x", g + 1 if nxt else g)
                    router_dots(g, 0)
                    router_dots(g, 1)
                if nxt:
                    projected(g + 1, 7)
                if attn:
                    router_dots(g, 2)
                if nxt2:
                    rank(g + 2, 0)
                    rank(g + 2, 1)
                if nxt:
                    projected(g + 1, 11)
                if attn:
                    router_logits(g)
                if nxt2:
                    rank(g + 2, 2)
                    rank(g + 2, 3)
                if nxt:
                    projected(g + 1, 15)
                if attn:
                    features(yT, 0, S["yt_pe"], g, S["yev_d"])
                if nxt2:
                    masks(g + 2)
                if nxt:
                    projected(g + 1, 19)

            dve.wait_ge(S["ld_const"], 16 * 4)
            v.tensor_tensor(gw[:, :], gw[:, :], wrow[:, :], ALU.mult).then_inc(S["c_gw"], 1)
            v.tensor_tensor_reduce(out=brow[:, :], in0=brow[:, :], in1=wrow[:, :], scale=1.0, scalar=0.0, op0=ALU.mult,
                                   op1=ALU.add, accum_out=score0[:, 0:1]).then_inc(S["c_bw"], 1)
            dve.wait_ge(S["c_bw"], 1)
            v.tensor_tensor(score0[:, 0:1], score0[:, 0:1], score0[:, 1:2], ALU.add).then_inc(S["c_s0"], 1)
            first = Group(None)
            dve.wait_ge(S["ld_bias"], 48)
            for e in range(E):
                v.tensor_copy(w_router[0:TT, e, :], rjunk[:, :, :].rearrange("q e d -> q (e d)")
                              .rearrange("q (d e) -> q d e", e=E)[:, :, e]).then_inc(S["c_rw"], 1)
            dve.wait_ge(S["c_rw"], E)
            dve.wait_ge(S["c_gw"], 1)
            dve.wait_ge(S["c_s0"], 1)
            score_stats(first)
            split_low(0)
            score_dots(first)
            split_low(1)
            dve.wait_ge(S["c_mask"], 2 + NP)
            for b in range(GB):
                rank(first, b)
            masks(first)
            for k in range(2, NPQ):
                split_low(k)
            dve.wait_ge(S["hev"], 2)
            ln_stats(h, first, "x")
            normalise(h, first, "x", "y", first + -1)
            score_stats(first + 1)
            features(xT, 3, S["xt_pe"], first, S["xev_d"])
            score_dots(first + 1)
            for n in DVE_OUT:
                projected(first, n)
                if n == 11:
                    for b in range(GB):
                        rank(first + 1, b)
            masks(first + 1)
            step(first, False, True, True)
            with dve.Fori(1, NG - 2) as i:
                step(Group(i), True, True, True)
            step(Group(None, NG - 2), True, True, False)
            step(Group(None, NG - 1), True, False, False)
            step(Group(None, NG), True, False, False, attn=False)

        @block.gpsimd
        def _(pool):
            q = nc.gpsimd

            q.memset(ident[:, :], 0.0).then_inc(S["c_ident"], 1)
            q.memset(earlier[:, :], 1.0).then_inc(S["c_mask"], 1)
            q.memset(neg_half[:, :], -0.5).then_inc(S["c_neg"], 1)
            q.memset(eps[:, :], LN_EPS).then_inc(S["c_neg"], 1)
            pool.wait_ge(S["c_ident"], 1)
            q.affine_select(out=ident[:, :], in_=ident[:, :], compare_op=ALU.not_equal, fill=1.0, base=0,
                            pattern=[[-1, 128]], channel_multiplier=1).then_inc(S["c_ident"], 1)
            pool.wait_ge(S["c_mask"], 1)
            q.affine_select(out=earlier[:, :], in_=earlier[:, :], compare_op=ALU.is_gt, fill=0.0, base=0,
                            pattern=[[-1, N]], channel_multiplier=1).then_inc(S["c_mask"], 1)
            for n, (b, t) in enumerate(PAIRS):
                q.iota(place[:, n, :], pattern=[[1, TT]], base=TT * t - KEEP * b,
                       channel_multiplier=0).then_inc(S["c_mask"], 1)
            for b in range(GB):
                q.memset(v1[:, b, :, DH], 1.0).then_inc(S["c_ones"], 1)
            pool.wait_ge(S["c_neg"], 2)

            def score_rstd(g):
                wait(pool, S["f_aggr"], g, GB, GB)
                wait(pool, S["f_scale"], g, 1, 0)
                q.tensor_tensor(rstd[:, :], mv[:, :, 1], eps[0:N, 0:GB], ALU.add).then_inc(S["f_eps"], 1)
                wait(pool, S["f_eps"], g, 1, 1)
                q.tensor_tensor(rstd[:, :], rstd[:, :], neg_half[0:N, 0:GB], ALU.pow).then_inc(S["f_rstd"], 1)

            def ln_rstd(g, k):
                wait(pool, S[k + "_aggr"], g, NT, NT)
                q.tensor_tensor(lrs[:, :], lmv[:, :, 1], eps[0:TT, 0:NT], ALU.add).then_inc(S[k + "_eps"], 1)
                wait(pool, S[k + "_eps"], g, 1, 1)
                q.tensor_tensor(lrs[:, :], lrs[:, :], neg_half[0:TT, 0:NT], ALU.pow).then_inc(S[k + "_rstd"], 1)

            def low_part(g, k):
                wait(pool, S[k + "_hi"], g, 1, 1)
                q.tensor_tensor(xs[:, :, D:D + D2], xn[:, :, D1:D], xs[:, :, D1:D].bitcast(F32), ALU.subtract)
                q.tensor_tensor(xs[:, :, 2 * 128:3 * 128], xn[:, :, 0:D1], xs[:, :, 0:D1].bitcast(F32),
                                ALU.subtract).then_inc(S[k + "_lo"], 1)

            def residual_bias(g):
                wait(pool, S["hev"], g, 2, 2)
                wait(pool, S["h2s"], g, 2, 0)
                q.tensor_tensor(hb[:, :, :], h[:, :, :], bias_o[0:TT, :].unsqueeze(1).to_broadcast([TT, NT, D]),
                                ALU.add).then_inc(S["hbs"], 1)

            def router_pick(g):
                wait(pool, S["rprob"], g, 1, 1)
                wait(pool, S["comb"], g, CS, 0)
                p0, p1, p2 = (pr[:, :, e] for e in range(E))
                q.tensor_tensor(cmp[:, :, 0], p0, p1, ALU.subtract)
                q.tensor_tensor(cmp[:, :, 1], p0, p2, ALU.subtract)
                q.tensor_tensor(cmp[:, :, 2], p1, p2, ALU.subtract).then_inc(S["rcmp"], 1)
                wait_apart(pool, S["rcmp"], g, 4, 1, S["passed_p"])
                q.tensor_scalar(cmp[:, :, 0:3], cmp[:, :, 0:3], 0.0, None, ALU.is_ge).then_inc(S["rcmp"], 1)
                wait_apart(pool, S["rcmp"], g, 4, 2, S["passed_p"])
                q.tensor_scalar(cmp[:, :, 3:6], cmp[:, :, 0:3], -1.0, 1.0, ALU.mult, ALU.add).then_inc(S["rcmp"], 1)
                wait(pool, S["rcmp"], g, 4, 3)
                q.tensor_tensor(keep[:, :, 0], cmp[:, :, 3], cmp[:, :, 4], ALU.mult)
                q.tensor_tensor(keep[:, :, 1], cmp[:, :, 0], cmp[:, :, 5], ALU.mult)
                q.tensor_tensor(keep[:, :, 2], cmp[:, :, 1], cmp[:, :, 2], ALU.mult).then_inc(S["rcmp"], 1)
                wait_apart(pool, S["rcmp"], g, 4, 4, S["passed_p"])
                q.tensor_scalar(keep[:, :, :], keep[:, :, :], -1.0, 1.0, ALU.mult, ALU.add).then_inc(S["rkeep"], 1)
                wait(pool, S["rkeep"], g, 4, 1)
                q.tensor_tensor(keep[:, :, :], keep[:, :, :], pr[:, :, :], ALU.mult).then_inc(S["rkeep"], 1)
                wait(pool, S["rkeep"], g, 4, 2)
                q.tensor_tensor(den[:, :, 0], keep[:, :, 0], keep[:, :, 1], ALU.add).then_inc(S["rkeep"], 1)
                wait(pool, S["rkeep"], g, 4, 3)
                q.tensor_tensor(den[:, :, 1], den[:, :, 0], keep[:, :, 2], ALU.add).then_inc(S["rkeep"], 1)
                wait(pool, S["rden_s"], g, 1, 1)
                q.tensor_tensor(cw[:, :, :], keep[:, :, :], rden[:, :].unsqueeze(2).to_broadcast([TT, NT, E]),
                                ALU.mult).then_inc(S["cws"], 1)

            def split_low(k):
                pool.wait_ge(S["w_his"], k + 1)
                q.tensor_tensor(w_lo[:, :, PIECE * k:PIECE * (k + 1)], stage[:, k % 2, :, :],
                                w_hi[:, :, PIECE * k:PIECE * (k + 1)].bitcast(F32), ALU.subtract).then_inc(S["w_los_p"], 1)

            def step(g, ffn, nxt, nxt2, attn=True):
                if ffn:
                    router_pick(g + -1)
                if nxt:
                    ln_rstd(g + 1, "x")
                    low_part(g + 1, "x")
                if nxt2:
                    score_rstd(g + 2)
                if attn:
                    ln_rstd(g, "y")
                if nxt:
                    residual_bias(g + 1)
                if attn:
                    low_part(g, "y")

            first = Group(None)
            score_rstd(first)
            pool.wait_ge(S["ld_bias"], 48)
            ln_rstd(first, "x")
            low_part(first, "x")
            score_rstd(first + 1)
            residual_bias(first)
            for k in range(NPQ, NPW):
                split_low(k)
            step(first, False, True, True)
            with pool.Fori(1, NG - 2) as i:
                step(Group(i), True, True, True)
            step(Group(None, NG - 2), True, True, False)
            step(Group(None, NG - 1), True, False, False)
            step(Group(None, NG), True, False, False, attn=False)


_INS = ['x', 'L0_tok_gamma', 'L0_tok_beta', 'L0_tok_w', 'L0_tok_b', 'L0_attn_w_qkv', 'L0_attn_w_out', 'L0_attn_b_out',
        'L0_ffn_shared_gate', 'L0_ffn_shared_up', 'L0_ffn_shared_down', 'L0_ffn_routed_gate', 'L0_ffn_routed_up',
        'L0_ffn_routed_down', 'L0_ffn_router_w', 'L0_ffn_routing_bias']
_OUTS = [((128, 87, 192), 'float32')]


def kernel(**inputs):
    import numpy as _np
    import concourse.bacc as _bacc
    from concourse import mybir as _mybir
    from concourse.bass_utils import run_bass_kernel_spmd as _run

    nc = _bacc.Bacc("TRN2", target_bir_lowering=False, num_devices=1)
    arrays, args = {}, []
    for name in _INS:
        a = _np.ascontiguousarray(inputs[name])
        arrays[f"in_{name}_dram"] = a
        args.append(nc.dram_tensor(f"in_{name}_dram", a.shape, _mybir.dt.from_np(a.dtype), kind="ExternalInput").ap())
    for i, (shape, dtype) in enumerate(_OUTS):
        dt = _mybir.dt.from_np(_np.dtype(dtype))
        args.append(nc.dram_tensor(f"out_{i}_dram", shape, dt, kind="ExternalOutput").ap())
    audio_tower_kernel(nc, *args)
    r = _run(nc, [arrays], core_ids=[0])
    return r.results[0]["out_0_dram"]
```

```python
from contextlib import ExitStack

import concourse.bass as bass
from concourse import mybir

ALU = mybir.AluOpType
ACT = mybir.ActivationFunctionType
F32 = mybir.dt.float32
F32R = mybir.dt.float32r
F16 = mybir.dt.float16
I16 = mybir.dt.int16
U32 = mybir.dt.uint32
AX_X = mybir.AxisListType.X

LN_EPS = 1e-5
HEADS = 12
DH = 64
TOPK = 2


class Group:

    def __init__(self, reg, off=0):
        self.reg, self.off = reg, off

    def __add__(self, n):
        return Group(self.reg, self.off + n)

    def count(self, per, k):
        fixed = self.off * per + k
        return fixed if self.reg is None else self.reg * per + fixed

    def index(self):
        return self.count(1, 0)


def wait(eng, sem, g, per, k):
    v = g.count(per, k)
    if not isinstance(v, int) or v > 0:
        eng.wait_ge(sem, v)


def wait_apart(eng, sem, g, per, k, passed):
    wait(eng, sem, g, per, k)
    eng.sem_inc(passed, 1)


def audio_tower_kernel(nc, x, gamma, beta, tok_w, tok_b, w_qkv, w_out, b_out, sh_gate, sh_up, sh_down,
                       rt_gate, rt_up, rt_down, router_w, routing_bias, out):
    B, N, D = x.shape
    KEEP = int(N * 0.7)
    GB = 4
    NG = B // GB
    TOK = GB * KEEP
    NT = 3
    TT = TOK // NT
    D1 = 128
    D2 = D - D1
    INNER = HEADS * DH
    E = rt_gate.shape[0]
    NE = E + 1
    I = sh_gate.shape[1]
    IC = I // 128
    HC = NE * IC
    QK = 2 * INNER // 128
    OC = INNER // 128
    HU = GB
    UNITS = HEADS
    PH = HEADS // 2
    VH = INNER // 2
    NV = 2 * NT
    NPR = NV + QK
    WC = 3 * INNER + NE * 2 * I
    PIECE = 2 * I
    NPQ = 3 * INNER // PIECE
    PIECES = [2, 0, 1]
    EP = [(e, k) for e in range(NE) for k in range(3)]
    assert 3 * INNER % PIECE == 0
    SCALE = DH ** -0.5
    assert TOK % NT == 0 and TOK <= 512 and NE * IC == UNITS and E == 3 and TOPK == 2

    PAIRS = [(b, t) for b in range(GB) for t in range(NT)
             if b * KEEP < (t + 1) * TT and (b + 1) * KEEP > t * TT]
    NP = len(PAIRS)

    with ExitStack() as ctx:
        def sb(name, shape, dt=F32):
            return ctx.enter_context(nc.sbuf_tensor(name, shape, dt))

        def sem(name):
            return ctx.enter_context(nc.semaphore(name))

        w_hi = sb("w_hi", [128, WC], F32R)
        w_lo = sb("w_lo", [128, WC], F32R)
        w_rest = sb("w_rest", [128, WC], F32R)
        w_down = sb("w_down", [128, NE, IC, 2 * D], F32R)
        w_o = sb("w_o", [128, OC, D])
        w_router = sb("w_router", [128, E, D])
        ident = sb("ident", [128, 128])
        earlier = sb("earlier", [N, N])
        place = sb("place", [N, NP, TT], I16)
        gw = sb("gw", [128, D])
        token = sb("token", [N, GB], F16)
        bias_o = sb("bias_o", [128, D])
        bias_r = sb("bias_r", [128, E])
        score0 = sb("score0", [128, 2])
        neg_half = sb("neg_half", [128, GB])
        eps = sb("eps", [128, GB])
        xt = sb("xt", [N, GB, D])
        bst = sb("bst", [N, GB, 6])
        mv = sb("mv", [N, GB, 2])
        rstd = sb("rstd", [N, GB])
        neg_mean = sb("neg_mean", [N, GB])
        score = sb("score", [N, 3, GB])
        rk = sb("rk", [N, 4, GB])
        row0 = sb("row0", [TT, NT])
        idx = sb("idx", [TT, NT], U32)
        mask = sb("mask", [N, NP, TT], F16)
        h = sb("h", [TT, NT, D])
        hb = sb("hb", [TT, NT, D])
        h2 = sb("h2", [TT, NT, D])
        acc = sb("acc", [TT, NT, 2 * D])
        xn = sb("xn", [TT, NT, D])
        xs = sb("xs", [TT, NT, 3 * 128], F32R)
        lst = sb("lst", [TT, NT, 6])
        lmv = sb("lmv", [TT, NT, 2])
        lrs = sb("lrs", [TT, NT])
        xT = sb("xT", [128, 4, TOK], F32R)
        yT = sb("yT", [128, 4, TOK], F32R)
        qk = sb("qk", [128, QK, TOK])
        oT = qk[:, 0:OC, :]
        v1 = sb("v1", [KEEP, GB, INNER])
        vt = sb("vt", [TT, NT, INNER])
        p_v = sb("p", [128, 2 * HU * KEEP])
        p = p_v[0:KEEP, :].rearrange("q (r a n) -> q r a n", r=2, a=HU)
        rjunk = p_v[0:TT, 0:2 * D].rearrange("q (r d) -> q r d", r=2)
        junk = p_v[0:N, 2 * D:2 * D + 2 * N].rearrange("q (r n) -> q r n", r=2)
        pT = sb("pT", [KEEP, 2, HU, KEEP])
        nmx = sb("nmx", [KEEP, 2, 2, HU])
        psum = sb("psum", [KEEP, 4, HU])
        rsum = sb("rsum", [KEEP, 4, HU])
        h_hi = sb("h_hi", [128, HC, TOK], F32R)
        h_lo = sb("h_lo", [128, HC, TOK], F32R)
        th_v = sb("th", [128, 4 * I])
        th = th_v[:, 0:4 * TOK].rearrange("p (r n) -> p r n", r=4)
        stage = qk[:, :, :].rearrange("p c n -> p (c n)")[:, 0:4 * PIECE].rearrange("p (r a n) -> p r a n", r=2, a=2)
        stage_e = th_v[:, :].rearrange("p (r n) -> p r n", r=2)
        spare = qk[:, :, :].rearrange("p c n -> p (c n)")[:, 4 * PIECE:4 * PIECE + (2 + E) * D]
        wrow, brow = spare[:, 0:D], spare[:, D:2 * D]
        rows_r = spare[0:TT, 2 * D:(2 + E) * D]
        z = sb("z", [TT, NT, E])
        ez = sb("ez", [TT, NT, E])
        pr = sb("pr", [TT, NT, E])
        cmp = sb("cmp", [TT, NT, 6])
        keep = sb("keep", [TT, NT, E])
        den = sb("den", [TT, NT, 2])
        rden = sb("rden", [TT, NT])
        cw = sb("cw", [TT, NT, E])

        ps = ctx.enter_context(nc.psum_tensor("ps", [128, 8, 512], F32))
        GU0 = 4

        names = """ld_const ld_bias ld_w0 ld_w1 ld_x st_out ld_small
            c_ident c_mask c_neg c_gw c_bw c_s0 c_rw w_his w_los e_his e_los e_rows ld_e0 ld_e1
            f_bn f_aggr f_negmu f_eps f_rstd f_xc f_dot f_scale f_score f_bc f_rank f_rk f_mask
            f_sel f_row f_idx ld_h ld_v hbs
            x_bn x_aggr x_eps x_rstd x_norm x_hi x_lo
            y_bn y_aggr y_eps y_rstd y_norm y_hi y_lo
            xt_pe xev_a xev_d prj prj_a prj_d
            s_pe snmx sexp srec pnm t_pe pte pv_pe oev_a oev_d wo_pe h2s
            yt_pe yev_a yev_d gate_pe up_pe tanhs silus hts h_his h_los dn_pe comb total
            passed_d passed_p passed_s
            rdot rz rexp rone rprob rcmp rkeep rden_s cws""".split()
        S = {n: sem("s_" + n) for n in names}

        def bank(k, parts, cols):
            return ps[0:parts, k, 0:cols]

        def qk_chunk(n):
            c, k = divmod(n - NV, 2)
            return OC * k + c

        DVE_OUT = [n for n in range(NPR) if n % 4 == 3]
        ACT_OUT = [n for n in range(NPR) if n % 4 != 3]
        assert all(n < NV or qk_chunk(n) >= OC for n in DVE_OUT)

        def copied(eng, g, n):
            d, a = sum(m <= n for m in DVE_OUT), sum(m <= n for m in ACT_OUT)
            wait(eng, S["prj_a"], g, len(ACT_OUT), a)
            wait(eng, S["prj_d"], g, len(DVE_OUT), d)

        TERMS = [(w_lo, 0), (w_hi, 3), (w_rest, 2), (w_rest, 1), (w_hi, 0)]
        CS = NE * NT

        def stage_of_rows(m):
            return stage_e[:, m % 2, :].rearrange("p (a n) -> p a n", a=2)

        def stage_of_down(m):
            return stage_e[:, m % 2, 0:IC * D].rearrange("p (c d) -> p c d", c=IC)

        def columns(m):
            e, k = EP[m]
            return slice(3 * INNER + (2 * e + k) * I, 3 * INNER + (2 * e + k + 1) * I)

        block = ctx.enter_context(nc.Block())

        @block.sync
        def _(sp):
            def bcast(dst, src, done):
                sp.dma_start(dst, src.partition_broadcast(128)).then_inc(S[done], 16)

            def load_x(g):
                v = g.index()
                src = x[v * GB:v * GB + GB] if isinstance(v, int) else x[bass.ds(v * GB, GB), :, :]
                sp.dma_start(xt[:, :, :], src.rearrange("b n d -> n b d")).then_inc(S["ld_x"], 16)

            def load_piece(k):
                if k >= 2:
                    sp.wait_ge(S["w_los"], k - 1)
                w = w_qkv[:, PIECE * PIECES[k]:PIECE * (PIECES[k] + 1)]
                sp.dma_start(stage[:, k % 2, 0, :], w[0:D1, :]).then_inc(S[f"ld_w{k % 2}"], 16)
                sp.dma_start(stage[0:D2, k % 2, 1, :], w[D1:D, :]).then_inc(S[f"ld_w{k % 2}"], 16)
                sp.dma_start(stage[D2:2 * D2, k % 2, 1, :], w[D1:D, :]).then_inc(S[f"ld_w{k % 2}"], 16)

            def load_experts_piece(m):
                if m >= 2:
                    sp.wait_ge(S["e_los"], m - 1)
                e, k = EP[m]
                if k == 2:
                    w = sh_down if e == 0 else rt_down[e - 1]
                    sp.dma_start(stage_of_down(m), w.rearrange("(c p) d -> p c d", p=128)).then_inc(S[f"ld_e{m % 2}"], 16)
                else:
                    w = (sh_gate, sh_up)[k] if e == 0 else (rt_gate, rt_up)[k][e - 1]
                    st = stage_of_rows(m)
                    sp.dma_start(st[:, 0, :], w[0:D1, :]).then_inc(S[f"ld_e{m % 2}"], 16)
                    sp.dma_start(st[0:D2, 1, :], w[D1:D, :]).then_inc(S[f"ld_e{m % 2}"], 16)
                    sp.dma_start(st[D2:2 * D2, 1, :], w[D1:D, :]).then_inc(S[f"ld_e{m % 2}"], 16)

            def store(g):
                wait_apart(sp, S["total"], g, 1, 1, S["passed_s"])
                v = g.index()
                flat = out.rearrange("b k d -> (b k) d")
                dst = flat[v * TOK:(v + 1) * TOK] if isinstance(v, int) else flat[bass.ds(v * TOK, TOK), :]
                sp.dma_start(dst.rearrange("(t q) d -> q t d", t=NT), acc[:, :, 0:D]).then_inc(S["st_out"], 16)

            def align_v(g):
                wait_apart(sp, S["prj_a"], g, len(ACT_OUT), sum(n < NV for n in ACT_OUT), S["passed_s"])
                wait_apart(sp, S["prj_d"], g, len(DVE_OUT), sum(n < NV for n in DVE_OUT), S["passed_s"])
                for b, t in PAIRS:
                    lo, hi = max(b * KEEP, t * TT), min((b + 1) * KEEP, (t + 1) * TT)
                    sp.dma_start(v1[lo - b * KEEP:hi - b * KEEP, b, :],
                                 vt[lo - t * TT:hi - t * TT, t, :]).then_inc(S["ld_v"], 16)

            load_x(Group(None))
            bcast(gw[:, :], gamma, "ld_const")
            bcast(wrow, tok_w, "ld_const")
            bcast(brow, beta, "ld_const")
            sp.dma_start(score0[:, 1:2], tok_b.partition_broadcast(128)).then_inc(S["ld_const"], 16)
            load_piece(0)
            load_piece(1)
            bcast(bias_o[:, :], b_out, "ld_bias")
            bcast(bias_r[:, :], routing_bias, "ld_bias")
            sp.dma_start(rows_r,
                         router_w.rearrange("d e -> (d e)").partition_broadcast(TT)).then_inc(S["ld_bias"], 16)
            for k in range(2, NPQ):
                load_piece(k)
            sp.dma_start(w_o[:, :, :], w_out.rearrange("(c p) d -> p c d", p=128)).then_inc(S["ld_small"], 16)
            sp.wait_ge(S["f_dot"], GB)
            load_x(Group(None, 1))
            load_experts_piece(0)
            load_experts_piece(1)
            align_v(Group(None))
            for m in range(2, len(EP)):
                load_experts_piece(m)

            def step(g, ffn, nxt, nxt2):
                if nxt2:
                    wait_apart(sp, S["f_dot"], g + 1, GB, GB, S["passed_s"])
                    load_x(g + 2)
                if ffn:
                    store(g + -1)
                if nxt:
                    align_v(g + 1)

            step(Group(None), False, True, True)
            step(Group(None, 1), True, True, True)
            with sp.Fori(2, NG - 2) as i:
                step(Group(i), True, True, True)
            step(Group(None, NG - 2), True, True, False)
            step(Group(None, NG - 1), True, False, False)
            store(Group(None, NG - 1))
            sp.wait_ge(S["st_out"], 16 * NG)

        @block.tensor
        def _(pe):
            mm = nc.tensor.matmul

            def rank_rows(g):
                wait(pe, S["f_score"], g, 1, 1)
                wait(pe, S["h2s"], g + -2, 2, 2)
                for b in range(GB):
                    last = mm(ps[0:N, 3, b * N:(b + 1) * N], score[:, 2, b:b + 1].to_broadcast([N, N]),
                              ident[0:N, 0:N], start=True, stop=True, is_transpose=True)
                last.then_inc(S["f_bc"], 1)

            def select(g):
                wait(pe, S["f_mask"], g, GB, GB)
                for t in range(NT):
                    mine = [n for n, (b, u) in enumerate(PAIRS) if u == t]
                    for n in mine:
                        last = mm(ps[0:TT, 3, 4 * t:4 * t + 1], mask[:, n, :], token[:, PAIRS[n][0]:PAIRS[n][0] + 1],
                                  start=(n == mine[0]), stop=(n == mine[-1]))
                last.then_inc(S["f_sel"], 1)

            def to_features(banks, done):
                for k in range(3):
                    for t in range(NT):
                        last = mm(ps[:, banks[k], t * TT:(t + 1) * TT], xs[:, t, 128 * k:128 * (k + 1)].bitcast(F32),
                                  ident[0:TT, 0:TT], start=True, stop=True, is_transpose=True)
                    last.then_inc(done, 1)

            def tokens_to_features(g):
                wait(pe, S["x_hi"], g, 1, 1)
                wait(pe, S["x_lo"], g, 1, 1)
                wait(pe, S["sexp"], g, HU * UNITS, 0)
                wait(pe, S["pte"], g, UNITS, 0)
                to_features((0, 1, 2), S["xt_pe"])

            def project(g, rows, experts):
                wait(pe, S["xev_a"], g, 2, 2)
                wait(pe, S["xev_d"], g, 1, 1)
                for n in range(NPR):
                    bk = GU0 + n % 4
                    if n < 4:
                        wait(pe, S["comb"], g + -2, CS, CS)
                    else:
                        m = n - 4
                        if m in DVE_OUT:
                            wait(pe, S["prj_d"], g, len(DVE_OUT), DVE_OUT.index(m) + 1)
                        else:
                            wait(pe, S["prj_a"], g, len(ACT_OUT), ACT_OUT.index(m) + 1)
                    if g.reg is None and g.off == 0 and n in (0, NV):
                        k = 1 if n == 0 else NPQ
                        pe.wait_ge(S["w_his"], k)
                        pe.wait_ge(S["w_los"], k)
                    if n >= NV:
                        c = qk_chunk(n)
                        dst = bank(bk, 128, TOK)
                    else:
                        t, f = divmod(n, 2)
                        dst = bank(bk, TT, VH)
                    for k, (w, xk) in enumerate(TERMS):
                        if n >= NV:
                            last = mm(dst, w[:, 128 * c:128 * (c + 1)], xT[:, xk, :], start=(k == 0), stop=(k == 4))
                        else:
                            c0 = 2 * INNER + VH * f
                            last = mm(dst, xT[:, xk, TT * t:TT * (t + 1)], w[:, c0:c0 + VH],
                                      start=(k == 0), stop=(k == 4))
                    last.then_inc(S["prj"], 1)
                    if n == 5 and rows is not None:
                        rank_rows(rows)
                    if n == 12 and experts is not None:
                        experts_to_features(experts)
                    if n == 15:
                        scores(g, 0)

            def scores(g, k):
                copied(pe, g, NV + 2 * k + 1)
                if k == 0:
                    wait(pe, S["yev_d"], g + -1, 1, 1)
                    wait(pe, S["yev_a"], g + -1, 2, 2)
                else:
                    wait(pe, S["sexp"], g, HU * UNITS, 2 * HU * k)
                for b in range(GB):
                    for odd in range(2):
                        rows, cols = slice(DH * odd, DH * (odd + 1)), slice(KEEP * b, KEEP * (b + 1))
                        last = mm(ps[0:KEEP, odd, cols], qk[rows, k, cols], qk[rows, OC + k, cols], start=True, stop=True)
                last.then_inc(S["s_pe"], 1)

            def transpose_p(g, u):
                wait(pe, S["pnm"], g, UNITS, u + 1)
                if u > 0:
                    wait(pe, S["pte"], g, UNITS, u)
                for b in range(GB):
                    last = mm(ps[0:KEEP, 2, b * KEEP:(b + 1) * KEEP], p[:, u % 2, b, :], ident[0:KEEP, 0:KEEP],
                              start=True, stop=True, is_transpose=True)
                last.then_inc(S["t_pe"], 1)

            def weigh_v(g, k, ranked=False):
                wait(pe, S["pte"], g, UNITS, 2 * k + 2)
                if k == 0:
                    wait(pe, S["ld_v"], g, 16 * NP, 16 * NP)
                if k == 0 and ranked:
                    wait(pe, S["f_idx"], g + 1, 1, 1)
                if k > 0:
                    wait(pe, S["oev_a" if k % 2 else "oev_d"], g, OC // 2, (k + 1) // 2)
                for b in range(GB):
                    for odd in range(2):
                        u = 2 * k + odd
                        last = mm(ps[DH * odd:DH * (odd + 1), 3, b * KEEP:(b + 1) * KEEP], v1[:, b, DH * u:DH * (u + 1)],
                                  pT[:, odd, b, :], start=True, stop=True)
                last.then_inc(S["pv_pe"], 1)

            def gate_up(g, c, projected):
                if c == 0:
                    wait(pe, S["yev_a"], g, 2, 2)
                    wait(pe, S["yev_d"], g, 1, 1)
                    if g.reg is None and g.off == 0:
                        pe.wait_ge(S["e_his"], len(EP))
                        pe.wait_ge(S["e_los"], len(EP))
                if c == 0 and not projected:
                    wait(pe, S["comb"], g, CS, 0)
                if c >= 2:
                    wait(pe, S["hts"], g, HC, c - 1)
                e, ic = divmod(c, IC)
                for up in range(2):
                    if c < 2 and projected:
                        m = NPR - 1 - (NPR - 1 - 2 * c - up) % 4
                        copied(pe, g + 1, m)
                    dst = bank(GU0 + 2 * (c % 2) + up, 128, TOK)
                    c0 = 3 * INNER + e * 2 * I + up * I + 128 * ic
                    for k, (w, xk) in enumerate(TERMS):
                        last = mm(dst, w[:, c0:c0 + 128], yT[:, xk, :], start=(k == 0), stop=(k == 4))
                    last.then_inc(S["up_pe" if up else "gate_pe"], 1)

            def down(g, n):
                e, t = divmod(n, NT)
                if n in (0, 2):
                    wait(pe, S["hts"], g, HC, HC - 1 + n // 2)
                if t == 0:
                    wait(pe, S["h_los"], g, HC, IC * (e + 1))
                if n >= 4:
                    wait(pe, S["comb"], g, CS, n - 3)
                dst = ps[0:TT, GU0 + n % 4, 0:2 * D]
                order = [(h_hi, 0), (h_lo, 0), (h_lo, 1), (h_hi, 1), (h_lo, 2), (h_hi, 2)]
                for k, (hs, c) in enumerate(order):
                    cols = 2 * D if hs is h_hi else 256
                    last = mm(dst[:, 0:cols], hs[:, e * IC + c, TT * t:TT * (t + 1)], w_down[:, e, c, 0:cols],
                              start=(k == 0), stop=(k == 5))
                last.then_inc(S["dn_pe"], 1)

            def project_out(g, nxt):
                wait(pe, S["oev_a"], g, OC // 2, OC // 2)
                wait(pe, S["oev_d"], g, OC // 2, OC // 2)
                if nxt:
                    wait(pe, S["xev_a"], g + 1, 2, 1)
                else:
                    wait(pe, S["sexp"], g, HU * UNITS, HU * UNITS)
                if g.reg is None and g.off == 0:
                    pe.wait_ge(S["ld_small"], 16)
                for t in range(NT):
                    dst = ps[0:TT, 3, t * D:(t + 1) * D] if t < NT - 1 else ps[0:TT, 0, 0:D]
                    for c in range(OC):
                        last = mm(dst, oT[:, c, TT * t:TT * (t + 1)], w_o[:, c, :], start=(c == 0), stop=(c == OC - 1))
                    if t >= NT - 2:
                        last.then_inc(S["wo_pe"], 1)

            def experts_to_features(g):
                wait(pe, S["y_hi"], g, 1, 1)
                wait(pe, S["y_lo"], g, 1, 1)
                wait(pe, S["h2s"], g, 2, 2)
                to_features((0, 2, 1), S["yt_pe"])

            def step(g, ffn, nxt, nxt2, attn=True):
                for k in range(PH + 1):
                    if attn and 0 < k < PH:
                        scores(g, k)
                    if nxt and k == 0:
                        select(g + 1)
                    if attn and k >= 1:
                        transpose_p(g, 2 * k - 2)
                    if ffn:
                        gate_up(g + -1, 2 * k, attn) if k < PH else down(g + -1, 0)
                        if k == PH:
                            down(g + -1, 1)
                    if attn and k >= 1:
                        transpose_p(g, 2 * k - 1)
                    if ffn:
                        gate_up(g + -1, 2 * k + 1, attn) if k < PH else down(g + -1, 2)
                        if k == PH:
                            down(g + -1, 3)
                    if attn and k >= 1:
                        weigh_v(g, k - 1, nxt)
                if nxt:
                    tokens_to_features(g + 1)
                if ffn:
                    for n in range(4, CS):
                        down(g + -1, n)
                if attn:
                    project_out(g, nxt)
                if nxt:
                    project(g + 1, g + 2 if nxt2 else None, g)
                elif attn:
                    experts_to_features(g)

            pe.wait_ge(S["c_ident"], 2)
            first = Group(None)
            rank_rows(first)
            select(first)
            tokens_to_features(first)
            project(first, first + 1, None)
            step(first, False, True, True)
            step(first + 1, True, True, True)
            with pe.Fori(2, NG - 2) as i:
                step(Group(i), True, True, True)
            step(Group(None, NG - 2), True, True, False)
            step(Group(None, NG - 1), True, False, False)
            step(Group(None, NG), True, False, False, attn=False)

        @block.scalar
        def _(act):
            af = nc.scalar.activation

            def split_weights(k):
                act.wait_ge(S[f"ld_w{k % 2}"], 16 * 3 * (k // 2 + 1))
                cols = slice(PIECE * PIECES[k], PIECE * (PIECES[k] + 1))
                af(w_hi[:, cols], stage[:, k % 2, 0, :], ACT.Copy)
                af(w_rest[:, cols], stage[:, k % 2, 1, :], ACT.Copy).then_inc(S["w_his"], 1)

            def split_experts(m):
                act.wait_ge(S[f"ld_e{m % 2}"], 16 * sum(1 if EP[i][1] == 2 else 3 for i in range(m % 2, m + 1, 2)))
                e, k = EP[m]
                if k == 2:
                    af(w_down[:, e, :, 0:D], stage_of_down(m), ACT.Copy).then_inc(S["e_his"], 1)
                else:
                    af(w_hi[:, columns(m)], stage_of_rows(m)[:, 0, :], ACT.Copy)
                    af(w_rest[:, columns(m)], stage_of_rows(m)[:, 1, :], ACT.Copy).then_inc(S["e_his"], 1)

            def high_part_tokens(g):
                wait(act, S["x_norm"], g, NT, NT)
                wait(act, S["yt_pe"], g + -1, 3, 0)
                af(xs[:, :, 0:D], xn[:, :, :], ACT.Copy).then_inc(S["x_hi"], 1)

            def high_part_experts(g, nxt):
                wait(act, S["y_norm"], g, NT, NT)
                if nxt:
                    wait(act, S["xt_pe"], g + 1, 3, 3)
                af(xs[:, :, 0:D], xn[:, :, :], ACT.Copy).then_inc(S["y_hi"], 1)

            def centre(g):
                wait(act, S["f_negmu"], g, 1, 1)
                for b in range(GB):
                    af(xt[:, b, :], xt[:, b, :], ACT.Identity, bias=neg_mean[:, b:b + 1]).then_inc(S["f_xc"], 1)

            def features(dst, k, bk, src, g, done):
                wait(act, src, g, 3, 1 if k == 0 else 3)
                af(dst[:, k, :], bank(bk, 128, TOK), ACT.Copy).then_inc(done, 1)

            def projected(g, n):
                wait(act, S["prj"], g, NPR, n + 1)
                if n >= NV:
                    af(qk[:, qk_chunk(n), :], bank(GU0 + n % 4, 128, TOK), ACT.Copy,
                       scale=-SCALE if qk_chunk(n) < OC else 1.0).then_inc(S["prj_a"], 1)
                else:
                    t, f = divmod(n, 2)
                    af(vt[:, t, VH * f:VH * (f + 1)], bank(GU0 + n % 4, TT, VH), ACT.Copy).then_inc(S["prj_a"], 1)

            def exponentials(g, u):
                wait(act, S["snmx"], g, PH, u // 2 + 1)
                if u >= 2:
                    wait(act, S["t_pe"], g, UNITS, u - 1)
                for b in range(GB):
                    af(p[:, u % 2, b, :], ps[0:KEEP, u % 2, b * KEEP:(b + 1) * KEEP], ACT.Exp, scale=-1.0,
                       bias=nmx[:, u // 2 % 2, u % 2, b:b + 1], accum_out=psum[:, u % 4, b:b + 1]).then_inc(S["sexp"], 1)

            def copy_pT(g, u):
                wait(act, S["t_pe"], g, UNITS, u + 1)
                if u >= 2:
                    wait(act, S["pv_pe"], g, PH, u // 2)
                af(pT[:, u % 2, :, :], bank(2, KEEP, HU * KEEP).rearrange("q (a n) -> q a n", a=HU),
                   ACT.Copy).then_inc(S["pte"], 1)

            def tanh_gate(g, c):
                wait(act, S["gate_pe"], g, HC, c + 1)
                if c >= 4:
                    wait(act, S["h_los"], g, HC, c - 3)
                af(th[:, c % 4, :], bank(GU0 + 2 * (c % 2), 128, TOK), ACT.Tanh, scale=0.5).then_inc(S["tanhs"], 1)

            def high_hidden(g, c):
                wait(act, S["hts"], g, HC, c + 1)
                af(h_hi[:, c, :], th[:, c % 4, :], ACT.Copy).then_inc(S["h_his"], 1)

            def out_features(g, c):
                wait(act, S["pv_pe"], g, PH, c + 1)
                af(oT[:, c, :], bank(3, 128, TOK), ACT.Copy).then_inc(S["oev_a"], 1)

            def router_exp(g):
                wait(act, S["rz"], g, 1, 1)
                af(ez[:, :, :], z[:, :, :], ACT.Exp, scale=-1.0).then_inc(S["rexp"], 1)

            def step(g, ffn, nxt, nxt2, attn=True):
                for k in range(PH + 1):
                    if nxt and k == 5:
                        high_part_tokens(g + 1)
                    if attn and k >= 1:
                        copy_pT(g, 2 * k - 2)
                    if attn and k < PH:
                        exponentials(g, 2 * k)
                    if ffn and k < PH:
                        tanh_gate(g + -1, 2 * k)
                    if attn and k >= 1:
                        copy_pT(g, 2 * k - 1)
                    if attn and k < PH:
                        exponentials(g, 2 * k + 1)
                    if ffn and k < PH:
                        tanh_gate(g + -1, 2 * k + 1)
                    if attn and k in (1, 3, 5):
                        out_features(g, k - 1)
                    if ffn and k >= 1:
                        high_hidden(g + -1, 2 * k - 1)
                    if ffn and k < PH:
                        high_hidden(g + -1, 2 * k)
                    if not ffn and k < PH:
                        split_experts(2 * k)
                        split_experts(2 * k + 1)
                if nxt:
                    features(xT, 0, 0, S["xt_pe"], g + 1, S["xev_a"])
                    features(xT, 3, 2, S["xt_pe"], g + 1, S["xev_a"])
                if nxt2:
                    centre(g + 2)
                if nxt:
                    for n in ACT_OUT[0:5]:
                        projected(g + 1, n)
                if attn:
                    high_part_experts(g, nxt)
                if nxt:
                    for n in ACT_OUT[5:10]:
                        projected(g + 1, n)
                if attn:
                    features(yT, 0, 0, S["yt_pe"], g, S["yev_a"])
                    features(yT, 3, 1, S["yt_pe"], g, S["yev_a"])
                if nxt:
                    for n in ACT_OUT[10:]:
                        projected(g + 1, n)
                if attn:
                    router_exp(g)

            first = Group(None)
            centre(first)
            for k in range(NPQ):
                split_weights(k)
            high_part_tokens(first)
            centre(first + 1)
            features(xT, 0, 0, S["xt_pe"], first, S["xev_a"])
            features(xT, 3, 2, S["xt_pe"], first, S["xev_a"])
            for n in ACT_OUT:
                projected(first, n)
            step(first, False, True, True)
            step(first + 1, True, True, True)
            with act.Fori(2, NG - 2) as i:
                step(Group(i), True, True, True)
            step(Group(None, NG - 2), True, True, False)
            step(Group(None, NG - 1), True, False, False)
            step(Group(None, NG), True, False, False, attn=False)

        @block.vector
        def _(dve):
            v = nc.vector

            def split_low(k):
                dve.wait_ge(S["w_his"], k + 1)
                cols = slice(PIECE * PIECES[k], PIECE * (PIECES[k] + 1))
                v.tensor_tensor(w_lo[:, cols], stage[:, k % 2, 0, :], w_hi[:, cols].bitcast(F32), ALU.subtract)
                v.tensor_tensor(w_rest[D2:2 * D2, cols], stage[D2:2 * D2, k % 2, 1, :],
                                w_rest[D2:2 * D2, cols].bitcast(F32), ALU.subtract).then_inc(S["w_los"], 1)

            def score_stats(g):
                wait(dve, S["ld_x"], g, 16, 16)
                for b in range(GB):
                    v.bn_stats(bst[:, b, :], xt[:, b, :]).then_inc(S["f_bn"], 1)
                wait(dve, S["f_bn"], g, GB, GB)
                wait_apart(dve, S["f_eps"], g, 1, 0, S["passed_d"])
                for b in range(GB):
                    v.bn_aggr(mv[:, b, :], bst[:, b, :]).then_inc(S["f_aggr"], 1)
                wait(dve, S["f_aggr"], g, GB, GB)
                wait(dve, S["f_xc"], g, GB, 0)
                v.tensor_scalar(neg_mean[:, :], mv[:, :, 0], -1.0, None, ALU.mult).then_inc(S["f_negmu"], 1)

            def score_dots(g):
                for b in range(GB):
                    wait(dve, S["f_xc"], g, GB, b + 1)
                    v.tensor_tensor_reduce(out=xt[:, b, :], in0=xt[:, b, :], in1=gw[0:N, :], scale=1.0, scalar=0.0,
                                           op0=ALU.mult, op1=ALU.add, accum_out=score[:, 0, b:b + 1]).then_inc(S["f_dot"], 1)
                wait(dve, S["f_dot"], g, GB, GB)
                wait(dve, S["f_rstd"], g, 1, 1)
                v.tensor_tensor(score[:, 1, :], score[:, 0, :], rstd[:, :], ALU.mult).then_inc(S["f_scale"], 1)
                wait(dve, S["f_scale"], g, 1, 1)
                v.tensor_scalar(score[:, 2, :], score[:, 1, :], score0[0:N, 0:1], None, ALU.add).then_inc(S["f_score"], 1)

            def rank(g, b):
                wait(dve, S["f_bc"], g, 1, 1)
                row = ps[0:N, 3, b * N:(b + 1) * N]
                s = score[:, 2, b:b + 1]
                wait(dve, S["f_rank"], g, 2 * GB, 2 * b - 1)
                v.tensor_scalar(junk[:, 0, :], row, s, None, ALU.is_gt, ALU.add,
                                accum_out=rk[:, 0, b:b + 1]).then_inc(S["f_rank"], 1)
                wait(dve, S["f_rank"], g, 2 * GB, 2 * b)
                v.scalar_tensor_tensor(out=junk[:, 1, :], in0=row, scalar=s, in1=earlier[:, :], op0=ALU.is_equal,
                                       op1=ALU.mult, accum_out=rk[:, 1, b:b + 1]).then_inc(S["f_rank"], 1)

            def masks(g):
                wait(dve, S["f_rank"], g, 2 * GB, 2 * GB)
                v.tensor_tensor(rk[:, 2, :], rk[:, 0, :], rk[:, 1, :], ALU.add).then_inc(S["f_rk"], 1)
                wait(dve, S["f_rk"], g, 3, 1)
                v.tensor_scalar(rk[:, 3, :], rk[:, 2, :], float(KEEP), 4096.0, ALU.is_ge, ALU.mult).then_inc(S["f_rk"], 1)
                wait(dve, S["f_rk"], g, 3, 2)
                v.tensor_tensor(rk[:, 3, :], rk[:, 3, :], rk[:, 2, :], ALU.add).then_inc(S["f_rk"], 1)
                wait(dve, S["f_rk"], g, 3, 3)
                wait(dve, S["f_sel"], g, 1, 0)
                for b in range(GB):
                    mine = [n for n, (c, t) in enumerate(PAIRS) if c == b]
                    of_b = slice(mine[0], mine[-1] + 1)
                    v.tensor_scalar(mask[:, of_b, :], place[:, of_b, :], rk[:, 3, b:b + 1], None,
                                    ALU.is_equal).then_inc(S["f_mask"], 1)

            def kept_numbers(g):
                wait(dve, S["f_sel"], g, 1, 1)
                wait(dve, S["f_row"], g, 1, 1)
                wait(dve, S["ld_h"], g, 16 * NT, 0)
                v.tensor_tensor(idx[:, :], ps[0:TT, 3, 0:4 * NT].rearrange("q (t c) -> q t c", c=4)[:, :, 0], row0[:, :],
                                ALU.add).then_inc(S["f_idx"], 1)
                wait(dve, S["f_idx"], g, 1, 1)
                v.tensor_scalar(row0[:, :], row0[:, :], float(GB * N), None, ALU.add).then_inc(S["f_row"], 1)

            def ln_stats(src, g, k):
                for t in range(NT):
                    ln_tile_stats(src, k, t)
                ln_moments(g, k)

            def ln_tile_stats(src, k, t):
                v.bn_stats(lst[:, t, :], src[:, t, :]).then_inc(S[k + "_bn"], 1)

            def ln_moments(g, k):
                wait_apart(dve, S[k + "_bn"], g, NT, NT, S["passed_d"])
                for t in range(NT):
                    v.bn_aggr(lmv[:, t, :], lst[:, t, :]).then_inc(S[k + "_aggr"], 1)

            def normalise(src, g, k, other, split):
                wait_to_normalise(g, k, other, split)
                for t in range(NT):
                    normalise_tile(src, k, t)

            def wait_to_normalise(g, k, other, split):
                wait(dve, S[k + "_rstd"], g, 1, 1)
                wait(dve, S[other + "_hi"], split, 1, 1)
                wait(dve, S[other + "_lo"], split, 1, 1)

            def normalise_tile(src, k, t):
                v.tensor_scalar(xn[:, t, :], src[:, t, :], lmv[:, t, 0:1], lrs[:, t:t + 1], ALU.subtract,
                                ALU.mult).then_inc(S[k + "_norm"], 1)

            def features(dst, bk, src, g, done):
                wait(dve, src, g, 3, 2)
                for part in range(2):
                    for to in range(2):
                        last = v.tensor_copy(dst[D2 * to:D2 * (to + 1), 1 + part, :],
                                             ps[D2 * part:D2 * (part + 1), bk, 0:TOK])
                last.then_inc(done, 1)

            def projected(g, n):
                wait(dve, S["prj"], g, NPR, n + 1)
                if n >= NV:
                    v.tensor_copy(qk[:, qk_chunk(n), :], bank(GU0 + n % 4, 128, TOK)).then_inc(S["prj_d"], 1)
                else:
                    t, f = divmod(n, 2)
                    v.tensor_copy(vt[:, t, VH * f:VH * (f + 1)], bank(GU0 + n % 4, TT, VH)).then_inc(S["prj_d"], 1)

            def row_max(g, k):
                wait(dve, S["s_pe"], g, PH, k + 1)
                if k >= 2:
                    wait(dve, S["sexp"], g, HU * UNITS, 2 * HU * (k - 1))
                v.tensor_reduce(nmx[:, k % 2, :, :], ps[0:KEEP, 0:2, 0:HU * KEEP].rearrange("q o (a m) -> q o a m", a=HU),
                                AX_X, ALU.min).then_inc(S["snmx"], 1)

            def normalise_weights(g, u):
                wait(dve, S["sexp"], g, HU * UNITS, HU * (u + 1))
                v.reciprocal(rsum[:, u % 4, :], psum[:, u % 4, :]).then_inc(S["srec"], 1)
                wait(dve, S["srec"], g, UNITS, u + 1)
                v.tensor_tensor(p[:, u % 2, :, :], p[:, u % 2, :, :],
                                rsum[:, u % 4, :].unsqueeze(2).to_broadcast([KEEP, HU, KEEP]),
                                ALU.mult).then_inc(S["pnm"], 1)

            def gated(g, c):
                wait(dve, S["tanhs"], g, HC, c + 1)
                t = th[:, c % 4, :]
                v.scalar_tensor_tensor(out=t, in0=t, scalar=1.0, in1=bank(GU0 + 2 * (c % 2), 128, TOK), op0=ALU.add,
                                       op1=ALU.mult).then_inc(S["silus"], 1)

            def hidden(g, c):
                wait(dve, S["silus"], g, HC, c + 1)
                wait(dve, S["up_pe"], g, HC, c + 1)
                v.scalar_tensor_tensor(out=th[:, c % 4, :], in0=th[:, c % 4, :], scalar=0.5,
                                       in1=bank(GU0 + 2 * (c % 2) + 1, 128, TOK),
                                       op0=ALU.mult, op1=ALU.mult).then_inc(S["hts"], 1)

            def out_features(g, c):
                wait(dve, S["pv_pe"], g, PH, c + 1)
                v.tensor_copy(oT[:, c, :], bank(3, 128, TOK)).then_inc(S["oev_d"], 1)

            def combine(g, n):
                e, t = divmod(n, NT)
                if n == 0:
                    wait(dve, S["cws"], g, 1, 1)
                    wait(dve, S["st_out"], g, 16, 0)
                wait(dve, S["dn_pe"], g, CS, n + 1)
                bk = ps[0:TT, GU0 + n % 4, 0:2 * D]
                a = acc[:, t, :]
                if e == 0:
                    v.tensor_tensor(a[:, 0:D], bk[:, 0:D], h2[:, t, :], ALU.add)
                    v.tensor_copy(a[:, D:2 * D], bk[:, D:2 * D]).then_inc(S["comb"], 1)
                else:
                    wait(dve, S["comb"], g, CS, n - NT + 1)
                    v.scalar_tensor_tensor(out=a, in0=bk, scalar=cw[:, t, e - 1:e], in1=a, op0=ALU.mult,
                                           op1=ALU.add).then_inc(S["comb"], 1)

            def residual(g):
                wait(dve, S["hbs"], g, 1, 1)
                wait(dve, S["wo_pe"], g, 2, 1)
                v.tensor_tensor(h2[:, 0:2, :], ps[0:TT, 3, 0:2 * D].rearrange("q (t d) -> q t d", t=2), hb[:, 0:2, :],
                                ALU.add).then_inc(S["h2s"], 1)
                wait(dve, S["wo_pe"], g, 2, 2)
                v.tensor_tensor(h2[:, 2, :], ps[0:TT, 0, 0:D], hb[:, 2, :], ALU.add).then_inc(S["h2s"], 1)
                wait(dve, S["h2s"], g, 2, 2)

            def router_dots(g, t):
                if t == 0:
                    wait(dve, S["y_norm"], g, NT, NT)
                for e in range(E):
                    n = t * E + e
                    wait(dve, S["rdot"], g, E * NT, n - 1)
                    v.tensor_tensor_reduce(out=rjunk[:, n % 2, :], in0=xn[:, t, :], in1=w_router[0:TT, e, :], scale=1.0,
                                           scalar=0.0, op0=ALU.mult, op1=ALU.add,
                                           accum_out=z[:, t, e:e + 1]).then_inc(S["rdot"], 1)

            def router_logits(g):
                wait(dve, S["rdot"], g, E * NT, E * NT)
                v.tensor_tensor(z[:, :, :], z[:, :, :], bias_r[0:TT, :].unsqueeze(1).to_broadcast([TT, NT, E]),
                                ALU.add).then_inc(S["rz"], 1)

            def router_probs(g):
                wait(dve, S["rexp"], g, 1, 1)
                v.tensor_scalar(ez[:, :, :], ez[:, :, :], 1.0, None, ALU.add).then_inc(S["rone"], 1)
                wait(dve, S["rone"], g, 1, 1)
                v.reciprocal(pr[:, :, :], ez[:, :, :]).then_inc(S["rprob"], 1)

            def router_share(g):
                wait(dve, S["rkeep"], g, 4, 4)
                v.reciprocal(rden[:, :], den[:, :, 1]).then_inc(S["rden_s"], 1)

            def step(g, ffn, nxt, nxt2, attn=True):
                for k in range(PH + 1):
                    if attn and k < PH:
                        row_max(g, k)
                    if ffn and k >= 1:
                        gated(g + -1, 2 * k - 1)
                        hidden(g + -1, 2 * k - 1)
                    if attn and k in (3, 5):
                        out_features(g, k - 2)
                    if nxt and k == 0:
                        kept_numbers(g + 1)
                    if attn and k < PH:
                        normalise_weights(g, 2 * k)
                    if k == (1 if attn else 0) and (g.reg is not None or g.off > 0):
                        router_probs(g + -1)
                    if ffn and k < PH:
                        gated(g + -1, 2 * k)
                    if ffn and k < PH:
                        hidden(g + -1, 2 * k)
                    if k == 2 and (g.reg is not None or g.off > 0):
                        router_share(g + -1)
                    if attn and k < PH:
                        normalise_weights(g, 2 * k + 1)
                    if nxt and k == 1:
                        wait(dve, S["ld_h"], g + 1, 16 * NT, 16 * NT)
                    if nxt and k in (1, 2, 3):
                        ln_tile_stats(h, "x", k - 1)
                    if nxt and k == 3:
                        ln_moments(g + 1, "x")
                    if nxt and k == 4:
                        wait_to_normalise(g + 1, "x", "y", g + -1)
                        normalise_tile(h, "x", 0)
                        normalise_tile(h, "x", 1)
                        normalise_tile(h, "x", 2)
                if ffn:
                    for n in range(4):
                        combine(g + -1, n)
                if attn:
                    out_features(g, OC - 1)
                if nxt:
                    features(xT, 1, S["xt_pe"], g + 1, S["xev_d"])
                if ffn:
                    for n in range(4, 7):
                        combine(g + -1, n)
                if nxt2:
                    score_stats(g + 2)
                if ffn:
                    for n in range(7, 10):
                        combine(g + -1, n)
                if nxt2:
                    score_dots(g + 2)
                if ffn:
                    for n in range(10, CS):
                        combine(g + -1, n)
                if attn:
                    residual(g)
                    ln_stats(h2, g, "y")
                if nxt:
                    projected(g + 1, 3)
                if attn:
                    normalise(h2, g, "y", "x", g + 1 if nxt else g)
                    router_dots(g, 0)
                    router_dots(g, 1)
                if nxt:
                    projected(g + 1, 7)
                if attn:
                    router_dots(g, 2)
                if nxt2:
                    rank(g + 2, 0)
                    rank(g + 2, 1)
                if nxt:
                    projected(g + 1, 11)
                if attn:
                    router_logits(g)
                if nxt2:
                    rank(g + 2, 2)
                    rank(g + 2, 3)
                if attn:
                    features(yT, 2, S["yt_pe"], g, S["yev_d"])
                if nxt:
                    projected(g + 1, 15)
                if nxt2:
                    masks(g + 2)

            dve.wait_ge(S["ld_const"], 16 * 4)
            v.tensor_tensor(gw[:, :], gw[:, :], wrow[:, :], ALU.mult).then_inc(S["c_gw"], 1)
            v.tensor_tensor_reduce(out=brow[:, :], in0=brow[:, :], in1=wrow[:, :], scale=1.0, scalar=0.0, op0=ALU.mult,
                                   op1=ALU.add, accum_out=score0[:, 0:1]).then_inc(S["c_bw"], 1)
            dve.wait_ge(S["c_bw"], 1)
            v.tensor_tensor(score0[:, 0:1], score0[:, 0:1], score0[:, 1:2], ALU.add).then_inc(S["c_s0"], 1)
            first = Group(None)
            dve.wait_ge(S["c_gw"], 1)
            dve.wait_ge(S["c_s0"], 1)
            score_stats(first)
            score_dots(first)
            dve.wait_ge(S["c_mask"], 2 + NP + 1)
            for b in range(GB):
                rank(first, b)
            masks(first)
            v.memset(row0[:, :], 0.0).then_inc(S["f_row"], 1)
            kept_numbers(first)
            split_low(0)
            split_low(1)
            dve.wait_ge(S["ld_bias"], 48)
            for e in range(E):
                v.tensor_copy(w_router[0:TT, e, :],
                              rows_r.rearrange("q (d e) -> q d e", e=E)[:, :, e]).then_inc(S["c_rw"], 1)
            dve.wait_ge(S["c_rw"], E)
            split_low(2)
            dve.wait_ge(S["ld_h"], 16 * NT)
            ln_stats(h, first, "x")
            normalise(h, first, "x", "y", first + -1)
            score_stats(first + 1)
            features(xT, 1, S["xt_pe"], first, S["xev_d"])
            score_dots(first + 1)
            for n in DVE_OUT:
                projected(first, n)
                if n == 11:
                    for b in range(GB):
                        rank(first + 1, b)
            masks(first + 1)
            step(first, False, True, True)
            step(first + 1, True, True, True)
            with dve.Fori(2, NG - 2) as i:
                step(Group(i), True, True, True)
            step(Group(None, NG - 2), True, True, False)
            step(Group(None, NG - 1), True, False, False)
            step(Group(None, NG), True, False, False, attn=False)

        @block.gpsimd
        def _(pool):
            q = nc.gpsimd

            q.memset(ident[:, :], 0.0).then_inc(S["c_ident"], 1)
            q.memset(earlier[:, :], 1.0).then_inc(S["c_mask"], 1)
            q.memset(neg_half[:, :], -0.5).then_inc(S["c_neg"], 1)
            q.memset(eps[:, :], LN_EPS).then_inc(S["c_neg"], 1)
            pool.wait_ge(S["c_ident"], 1)
            q.affine_select(out=ident[:, :], in_=ident[:, :], compare_op=ALU.not_equal, fill=1.0, base=0,
                            pattern=[[-1, 128]], channel_multiplier=1).then_inc(S["c_ident"], 1)
            pool.wait_ge(S["c_mask"], 1)
            q.affine_select(out=earlier[:, :], in_=earlier[:, :], compare_op=ALU.is_gt, fill=0.0, base=0,
                            pattern=[[-1, N]], channel_multiplier=1).then_inc(S["c_mask"], 1)
            for n, (b, t) in enumerate(PAIRS):
                q.iota(place[:, n, :], pattern=[[1, TT]], base=TT * t - KEEP * b,
                       channel_multiplier=0).then_inc(S["c_mask"], 1)
            q.iota(token[:, :], pattern=[[N, GB]], base=0, channel_multiplier=1,
                   allow_small_or_imprecise_dtypes=True).then_inc(S["c_mask"], 1)
            pool.wait_ge(S["c_neg"], 2)

            def score_rstd(g):
                wait(pool, S["f_aggr"], g, GB, GB)
                wait(pool, S["f_scale"], g, 1, 0)
                q.tensor_tensor(rstd[:, :], mv[:, :, 1], eps[0:N, 0:GB], ALU.add).then_inc(S["f_eps"], 1)
                wait(pool, S["f_eps"], g, 1, 1)
                q.tensor_tensor(rstd[:, :], rstd[:, :], neg_half[0:N, 0:GB], ALU.pow).then_inc(S["f_rstd"], 1)

            def ln_rstd(g, k):
                wait(pool, S[k + "_aggr"], g, NT, NT)
                q.tensor_tensor(lrs[:, :], lmv[:, :, 1], eps[0:TT, 0:NT], ALU.add).then_inc(S[k + "_eps"], 1)
                wait(pool, S[k + "_eps"], g, 1, 1)
                q.tensor_tensor(lrs[:, :], lrs[:, :], neg_half[0:TT, 0:NT], ALU.pow).then_inc(S[k + "_rstd"], 1)

            def low_part(g, k):
                wait(pool, S[k + "_hi"], g, 1, 1)
                q.tensor_tensor(xs[:, :, D:D + D2], xn[:, :, D1:D], xs[:, :, D1:D].bitcast(F32), ALU.subtract)
                q.tensor_tensor(xs[:, :, 2 * 128:3 * 128], xn[:, :, 0:D1], xs[:, :, 0:D1].bitcast(F32),
                                ALU.subtract).then_inc(S[k + "_lo"], 1)

            def gather(g):
                wait(pool, S["f_idx"], g, 1, 1)
                wait(pool, S["hbs"], g, 1, 0)
                wait_apart(pool, S["x_norm"], g, NT, 0, S["passed_p"])
                for t in range(NT):
                    pool.indirect_dma_start(h[:, t, :], None, x.rearrange("b n d -> (b n) d"),
                                            bass.IndirectOffsetOnAxis(ap=idx[:, t:t + 1], axis=0)).then_inc(S["ld_h"], 16)

            def residual_bias(g):
                wait(pool, S["ld_h"], g, 16 * NT, 16 * NT)
                wait(pool, S["h2s"], g, 2, 0)
                q.tensor_tensor(hb[:, :, :], h[:, :, :], bias_o[0:TT, :].unsqueeze(1).to_broadcast([TT, NT, D]),
                                ALU.add).then_inc(S["hbs"], 1)

            def router_pick(g):
                wait(pool, S["rprob"], g, 1, 1)
                wait(pool, S["comb"], g, CS, 0)
                p0, p1, p2 = (pr[:, :, e] for e in range(E))
                q.tensor_tensor(cmp[:, :, 0], p0, p1, ALU.subtract)
                q.tensor_tensor(cmp[:, :, 1], p0, p2, ALU.subtract)
                q.tensor_tensor(cmp[:, :, 2], p1, p2, ALU.subtract).then_inc(S["rcmp"], 1)
                wait_apart(pool, S["rcmp"], g, 4, 1, S["passed_p"])
                q.tensor_scalar(cmp[:, :, 0:3], cmp[:, :, 0:3], 0.0, None, ALU.is_ge).then_inc(S["rcmp"], 1)
                wait_apart(pool, S["rcmp"], g, 4, 2, S["passed_p"])
                q.tensor_scalar(cmp[:, :, 3:6], cmp[:, :, 0:3], -1.0, 1.0, ALU.mult, ALU.add).then_inc(S["rcmp"], 1)
                wait(pool, S["rcmp"], g, 4, 3)
                q.tensor_tensor(keep[:, :, 0], cmp[:, :, 3], cmp[:, :, 4], ALU.mult)
                q.tensor_tensor(keep[:, :, 1], cmp[:, :, 0], cmp[:, :, 5], ALU.mult)
                q.tensor_tensor(keep[:, :, 2], cmp[:, :, 1], cmp[:, :, 2], ALU.mult).then_inc(S["rcmp"], 1)
                wait_apart(pool, S["rcmp"], g, 4, 4, S["passed_p"])
                q.tensor_scalar(keep[:, :, :], keep[:, :, :], -1.0, 1.0, ALU.mult, ALU.add).then_inc(S["rkeep"], 1)
                wait(pool, S["rkeep"], g, 4, 1)
                q.tensor_tensor(keep[:, :, :], keep[:, :, :], pr[:, :, :], ALU.mult).then_inc(S["rkeep"], 1)
                wait(pool, S["rkeep"], g, 4, 2)
                q.tensor_tensor(den[:, :, 0], keep[:, :, 0], keep[:, :, 1], ALU.add).then_inc(S["rkeep"], 1)
                wait(pool, S["rkeep"], g, 4, 3)
                q.tensor_tensor(den[:, :, 1], den[:, :, 0], keep[:, :, 2], ALU.add).then_inc(S["rkeep"], 1)
                wait(pool, S["rden_s"], g, 1, 1)
                q.tensor_tensor(cw[:, :, :], keep[:, :, :], rden[:, :].unsqueeze(2).to_broadcast([TT, NT, E]),
                                ALU.mult).then_inc(S["cws"], 1)

            def split_low(m):
                pool.wait_ge(S["e_his"], m + 1)
                e, k = EP[m]
                if k == 2:
                    q.tensor_tensor(w_down[:, e, :, D:2 * D], stage_of_down(m), w_down[:, e, :, 0:D].bitcast(F32),
                                    ALU.subtract).then_inc(S["e_los"], 1)
                else:
                    cols = columns(m)
                    q.tensor_tensor(w_lo[:, cols], stage_of_rows(m)[:, 0, :], w_hi[:, cols].bitcast(F32),
                                    ALU.subtract).then_inc(S["e_rows"], 1)
                    pool.wait_ge(S["e_rows"], 2 * e + k + 1)
                    q.tensor_tensor(w_rest[D2:2 * D2, cols], stage_of_rows(m)[D2:2 * D2, 1, :],
                                    w_rest[D2:2 * D2, cols].bitcast(F32), ALU.subtract).then_inc(S["e_los"], 1)
                    pool.wait_ge(S["e_los"], m + 1)

            def low_hidden(g, c):
                wait(pool, S["h_his"], g, HC, c + 1)
                q.tensor_tensor(h_lo[:, c, :], th[:, c % 4, :], h_hi[:, c, :].bitcast(F32),
                                ALU.subtract).then_inc(S["h_los"], 1)

            def total(g):
                wait(pool, S["comb"], g, CS, CS)
                q.tensor_tensor(acc[:, :, 0:D], acc[:, :, 0:D], acc[:, :, D:2 * D], ALU.add).then_inc(S["total"], 1)

            def step(g, ffn, nxt, nxt2, attn=True):
                if nxt:
                    gather(g + 1)
                if ffn:
                    for c in range(3):
                        low_hidden(g + -1, c)
                    router_pick(g + -1)
                    for c in range(3, 7):
                        low_hidden(g + -1, c)
                else:
                    wait(pool, S["ld_h"], g + 1, 16 * NT, 16 * NT)
                    for m in range(8):
                        split_low(m)
                if nxt:
                    ln_rstd(g + 1, "x")
                if ffn:
                    for c in range(7, HC - 1):
                        low_hidden(g + -1, c)
                else:
                    for m in range(8, len(EP)):
                        split_low(m)
                if nxt:
                    low_part(g + 1, "x")
                if ffn:
                    low_hidden(g + -1, HC - 1)
                if nxt2:
                    score_rstd(g + 2)
                if ffn:
                    total(g + -1)
                if attn:
                    ln_rstd(g, "y")
                if nxt:
                    residual_bias(g + 1)
                if attn:
                    low_part(g, "y")

            first = Group(None)
            score_rstd(first)
            pool.wait_ge(S["ld_bias"], 48)
            gather(first)
            ln_rstd(first, "x")
            low_part(first, "x")
            score_rstd(first + 1)
            residual_bias(first)
            step(first, False, True, True)
            step(first + 1, True, True, True)
            with pool.Fori(2, NG - 2) as i:
                step(Group(i), True, True, True)
            step(Group(None, NG - 2), True, True, False)
            step(Group(None, NG - 1), True, False, False)
            step(Group(None, NG), True, False, False, attn=False)


_INS = ['x', 'L0_tok_gamma', 'L0_tok_beta', 'L0_tok_w', 'L0_tok_b', 'L0_attn_w_qkv', 'L0_attn_w_out', 'L0_attn_b_out',
        'L0_ffn_shared_gate', 'L0_ffn_shared_up', 'L0_ffn_shared_down', 'L0_ffn_routed_gate', 'L0_ffn_routed_up',
        'L0_ffn_routed_down', 'L0_ffn_router_w', 'L0_ffn_routing_bias']
_OUTS = [((128, 87, 192), 'float32')]


def kernel(**inputs):
    import numpy as _np
    import concourse.bacc as _bacc
    from concourse import mybir as _mybir
    from concourse.bass_utils import run_bass_kernel_spmd as _run

    nc = _bacc.Bacc("TRN2", target_bir_lowering=False, num_devices=1)
    arrays, args = {}, []
    for name in _INS:
        a = _np.ascontiguousarray(inputs[name])
        arrays[f"in_{name}_dram"] = a
        args.append(nc.dram_tensor(f"in_{name}_dram", a.shape, _mybir.dt.from_np(a.dtype), kind="ExternalInput").ap())
    for i, (shape, dtype) in enumerate(_OUTS):
        dt = _mybir.dt.from_np(_np.dtype(dtype))
        args.append(nc.dram_tensor(f"out_{i}_dram", shape, dt, kind="ExternalOutput").ap())
    audio_tower_kernel(nc, *args)
    r = _run(nc, [arrays], core_ids=[0])
    return r.results[0]["out_0_dram"]
```
